# Optimizing a Trainium2 kernel written in Bass

```python
import numpy as np
import jax
import jax.numpy as jnp

def _softmax(x, axis=-1):
    return jax.nn.softmax(x, axis=axis)

def _gelu(x):
    return jax.nn.gelu(x, approximate=True)

def _silu(x):
    return jax.nn.silu(x)

def _sigmoid(x):
    return jax.nn.sigmoid(x)

def _layernorm(x, axis=-1, eps=1e-05):
    m = jnp.mean(x, axis=axis, keepdims=True)
    v = jnp.var(x, axis=axis, keepdims=True)
    return (x - m) / jnp.sqrt(v + eps)

def _scatter_add(tgt, idx, src, axis=0):
    return tgt.at[idx].add(src)

def _segment_sum(src, seg, n):
    return jax.ops.segment_sum(src, seg, n)
kernel_name = 'mk_xattn_ffn_d1_seqx_r4_0d4963'

def setup_inputs(seed: int=0):
    np.random.seed(seed)
    _w = jnp.asarray

    def _rec_inputs():
        import jax
        import jax.numpy as jnp
        _rk = jax.random.key(seed)
        x = -0.0002928 + 1 * jax.random.normal(jax.random.fold_in(_rk, 1), (16, 128, 256), jnp.float32)
        _lenS = 128 - jax.random.randint(jax.random.fold_in(_rk, 7), (16,), 0, max(1, 128 // 4) + 1, jnp.int32)
        _lenS2 = 128 - jax.random.randint(jax.random.fold_in(_rk, 8), (16,), 0, max(1, 128 // 4) + 1, jnp.int32)
        _ctx_1024P = jax.random.normal(jax.random.fold_in(_rk, 11), (16, 16, 256), jnp.float32)
        _ctx_1024c = jax.random.dirichlet(jax.random.fold_in(_rk, 511), 0.3 * jnp.ones((16,), jnp.float32), (16, 128))
        _ctx_1024t = jnp.einsum('bsk,bkd->bsd', _ctx_1024c, _ctx_1024P)
        _ctx_1024t = _ctx_1024t * jax.lax.rsqrt(jnp.mean(jnp.square(_ctx_1024t)) + 1e-12) * 0.953939
        ctx_1024 = -1.39393e-06 + 0.999914 * (_ctx_1024t + 0.3 * jax.random.normal(jax.random.fold_in(_rk, 611), (16, 128, 256), jnp.float32))
        return (x, ctx_1024)
    x, ctx_1024 = _rec_inputs()

    def _L0_xattn_setup():
        import jax, jax.numpy as jnp
        import numpy as np
        D_MODEL = 256
        HEAD = 16
        key = jax.random.key(seed)
        ks = jax.random.split(key, 11)
        B, S, D = (2, 512, D_MODEL)
        s = 1.0 / np.sqrt(D)
        return {'query': jax.random.normal(ks[0], (B, S, D), jnp.float32), 'value': jax.random.normal(ks[1], (B, S, D), jnp.float32), 'key': jax.random.normal(ks[2], (B, S, D), jnp.float32), 'Wq_w': jax.random.normal(ks[3], (D, D), jnp.float32) * s, 'Wq_b': jnp.zeros((D,), jnp.float32), 'Wk_w': jax.random.normal(ks[4], (D, D), jnp.float32) * s, 'Wk_b': jnp.zeros((D,), jnp.float32), 'Wv_w': jax.random.normal(ks[5], (D, D), jnp.float32) * s, 'Wv_b': jnp.zeros((D,), jnp.float32), 'Wo_w': jax.random.normal(ks[6], (D, D), jnp.float32) * s, 'Wo_b': jnp.zeros((D,), jnp.float32)}
    _L0_xattn_all = _L0_xattn_setup()
    _L0_xattn_in = {k: v for k, v in _L0_xattn_all.items() if k in ('Wq_w', 'Wq_b', 'Wk_w', 'Wk_b', 'Wv_w', 'Wv_b', 'Wo_w', 'Wo_b')}
    del _L0_xattn_all

    def _L0_ffn_setup():
        import jax, jax.numpy as jnp
        import numpy as np
        DIM = 256
        DEPTH = 2
        HEADS = 8
        DIM_HEAD = 64
        WINDOW = 128
        INNER = HEADS * DIM_HEAD
        HID = int(DIM * 4 * 2 / 3)
        B, N = (2, 2048)
        QK_SCALE = 8.0

        def shift_token(t):
            t1, t2 = jnp.split(t, 2, axis=-1)
            t2 = jnp.pad(t2, ((0, 0), (1, 0), (0, 0)))[:, :-1]
            return jnp.concatenate([t1, t2], axis=-1)

        def l2norm(t):
            return t / jnp.clip(jnp.linalg.norm(t, axis=-1, keepdims=True), 1e-12)

        def rotate_half(x):
            x1, x2 = jnp.split(x, 2, axis=-1)
            return jnp.concatenate([-x2, x1], axis=-1)

        def rotary_xpos(q, k):
            n = q.shape[-2]
            half_idx = jnp.arange(0, DIM_HEAD, 2, dtype=jnp.float32)
            inv_freq = 1.0 / 10000.0 ** (half_idx / DIM_HEAD)
            t = jnp.arange(n, dtype=jnp.float32)
            freqs = t[:, None] * inv_freq[None, :]
            freqs = jnp.concatenate([freqs, freqs], axis=-1)
            base = (half_idx + 0.4 * DIM_HEAD) / (1.4 * DIM_HEAD)
            power = (t - n // 2) / float(WINDOW // 2)
            scale = base[None, :] ** power[:, None]
            scale = jnp.concatenate([scale, scale], axis=-1)
            cos, sin = (jnp.cos(freqs), jnp.sin(freqs))
            q = q * cos * scale + rotate_half(q) * sin * scale
            k = k * cos / scale + rotate_half(k) * sin / scale
            return (q, k)

        def local_attention(q, k, v):
            b, h, n, d = q.shape
            w = n // WINDOW
            bq = q.reshape(b, h, w, WINDOW, d) * QK_SCALE
            bk = k.reshape(b, h, w, WINDOW, d)
            bv = v.reshape(b, h, w, WINDOW, d)

            def look_around(t):
                p = jnp.pad(t, ((0, 0), (0, 0), (1, 0), (0, 0), (0, 0)))
                return jnp.concatenate([p[:, :, :w], p[:, :, 1:]], axis=3)
            bk, bv = (look_around(bk), look_around(bv))
            bt = jnp.arange(n).reshape(w, WINDOW)
            btp = jnp.pad(bt, ((1, 0), (0, 0)), constant_values=-1)
            btk = jnp.concatenate([btp[:w], btp[1:]], axis=1)
            sim = jnp.einsum('bhwid,bhwjd->bhwij', bq, bk)
            i = bt[:, :, None]
            j = btk[:, None, :]
            mask = (i < j) | (i > j + WINDOW) | (j == -1)
            sim = jnp.where(mask, -jnp.finfo(sim.dtype).max, sim)
            attn = jax.nn.softmax(sim, axis=-1)
            out = jnp.einsum('bhwij,bhwjd->bhwid', attn, bv)
            return out.reshape(b, h, n, d)

        def _layer(x, wqkv, qs, ksc, wo, lg, lb, w1, b1, w2, b2):
            b, n, _ = x.shape
            h = shift_token(x)
            qkv = h @ wqkv
            q, k, v = jnp.split(qkv, 3, axis=-1)
            to_heads = lambda t: t.reshape(b, n, HEADS, DIM_HEAD).transpose(0, 2, 1, 3)
            q, k, v = (to_heads(q), to_heads(k), to_heads(v))
            q = l2norm(q) * qs
            k = l2norm(k) * ksc
            q, k = rotary_xpos(q, k)
            o = local_attention(q, k, v)
            o = o.transpose(0, 2, 1, 3).reshape(b, n, INNER)
            x = x + o @ wo
            h = shift_token(x)
            mu = h.mean(-1, keepdims=True)
            var = h.var(-1, keepdims=True)
            h = (h - mu) / jnp.sqrt(var + 1e-05) * lg + lb
            h = h @ w1 + b1
            a, g = jnp.split(h, 2, axis=-1)
            h = a * jax.nn.gelu(g, approximate=False)
            x = x + h @ w2 + b2
            return x
        key = jax.random.key(seed)
        ks = jax.random.split(key, 6)
        return {'x': jax.random.normal(ks[0], (B, N, DIM), jnp.float32), 'wqkv': jax.random.normal(ks[1], (DEPTH, DIM, 3 * INNER), jnp.float32) * 0.02, 'q_scale': jnp.ones((DEPTH, DIM_HEAD), jnp.float32), 'k_scale': jnp.ones((DEPTH, DIM_HEAD), jnp.float32), 'wo': jax.random.normal(ks[2], (DEPTH, INNER, DIM), jnp.float32) * 0.02, 'ln_g': jnp.ones((DEPTH, DIM), jnp.float32), 'ln_b': jnp.zeros((DEPTH, DIM), jnp.float32), 'w1': jax.random.normal(ks[3], (DEPTH, DIM, 2 * HID), jnp.float32) * 0.02, 'b1': jnp.zeros((DEPTH, 2 * HID), jnp.float32), 'w2': jax.random.normal(ks[4], (DEPTH, HID, DIM), jnp.float32) * 0.02, 'b2': jnp.zeros((DEPTH, DIM), jnp.float32)}
    _L0_ffn_all = _L0_ffn_setup()
    _L0_ffn_in = {k: v for k, v in _L0_ffn_all.items() if k in ('wqkv', 'q_scale', 'k_scale', 'wo', 'ln_g', 'ln_b', 'w1', 'b1', 'w2', 'b2')}
    del _L0_ffn_all
    return {'x': x, 'ctx_1024': ctx_1024, 'L0_xattn_Wq_w': _L0_xattn_in['Wq_w'], 'L0_xattn_Wq_b': _L0_xattn_in['Wq_b'], 'L0_xattn_Wk_w': _L0_xattn_in['Wk_w'], 'L0_xattn_Wk_b': _L0_xattn_in['Wk_b'], 'L0_xattn_Wv_w': _L0_xattn_in['Wv_w'], 'L0_xattn_Wv_b': _L0_xattn_in['Wv_b'], 'L0_xattn_Wo_w': _L0_xattn_in['Wo_w'], 'L0_xattn_Wo_b': _L0_xattn_in['Wo_b'], 'L0_ffn_wqkv': _L0_ffn_in['wqkv'], 'L0_ffn_q_scale': _L0_ffn_in['q_scale'], 'L0_ffn_k_scale': _L0_ffn_in['k_scale'], 'L0_ffn_wo': _L0_ffn_in['wo'], 'L0_ffn_ln_g': _L0_ffn_in['ln_g'], 'L0_ffn_ln_b': _L0_ffn_in['ln_b'], 'L0_ffn_w1': _L0_ffn_in['w1'], 'L0_ffn_b1': _L0_ffn_in['b1'], 'L0_ffn_w2': _L0_ffn_in['w2'], 'L0_ffn_b2': _L0_ffn_in['b2']}

def reference(x, ctx_1024, L0_xattn_Wq_w, L0_xattn_Wq_b, L0_xattn_Wk_w, L0_xattn_Wk_b, L0_xattn_Wv_w, L0_xattn_Wv_b, L0_xattn_Wo_w, L0_xattn_Wo_b, L0_ffn_wqkv, L0_ffn_q_scale, L0_ffn_k_scale, L0_ffn_wo, L0_ffn_ln_g, L0_ffn_ln_b, L0_ffn_w1, L0_ffn_b1, L0_ffn_w2, L0_ffn_b2):
    import jax
    import jax.numpy as jnp

    def _L0_xattn_ref(query, value, key, Wq_w, Wq_b, Wk_w, Wk_b, Wv_w, Wv_b, Wo_w, Wo_b):
        import jax, jax.numpy as jnp
        import numpy as np
        D_MODEL = 256
        HEAD = 16
        B, S, D = query.shape
        H = HEAD
        kd = D // H
        Q = query @ Wq_w.T + Wq_b
        K = key @ Wk_w.T + Wk_b
        V = value @ Wv_w.T + Wv_b
        Q = Q.reshape(B, S, H, kd).transpose(0, 2, 1, 3)
        K = K.reshape(B, S, H, kd).transpose(0, 2, 1, 3)
        V = V.reshape(B, S, H, kd).transpose(0, 2, 1, 3)
        scale = 1.0 / jnp.sqrt(jnp.asarray(kd, query.dtype))
        score = jnp.einsum('bhqd,bhkd->bhqk', Q, K) * scale
        attn = jax.nn.softmax(score, axis=-1)
        x = jnp.einsum('bhqk,bhkd->bhqd', attn, V)
        x = x.transpose(0, 2, 1, 3).reshape(B, S, D)
        return x @ Wo_w.T + Wo_b

    def _L0_ffn_ref(x, wqkv, q_scale, k_scale, wo, ln_g, ln_b, w1, b1, w2, b2):
        import jax, jax.numpy as jnp
        import numpy as np
        DIM = 256
        DEPTH = 2
        HEADS = 8
        DIM_HEAD = 64
        WINDOW = 128
        INNER = HEADS * DIM_HEAD
        HID = int(DIM * 4 * 2 / 3)
        B, N = (2, 2048)
        QK_SCALE = 8.0

        def shift_token(t):
            t1, t2 = jnp.split(t, 2, axis=-1)
            t2 = jnp.pad(t2, ((0, 0), (1, 0), (0, 0)))[:, :-1]
            return jnp.concatenate([t1, t2], axis=-1)

        def l2norm(t):
            return t / jnp.clip(jnp.linalg.norm(t, axis=-1, keepdims=True), 1e-12)

        def rotate_half(x):
            x1, x2 = jnp.split(x, 2, axis=-1)
            return jnp.concatenate([-x2, x1], axis=-1)

        def rotary_xpos(q, k):
            n = q.shape[-2]
            half_idx = jnp.arange(0, DIM_HEAD, 2, dtype=jnp.float32)
            inv_freq = 1.0 / 10000.0 ** (half_idx / DIM_HEAD)
            t = jnp.arange(n, dtype=jnp.float32)
            freqs = t[:, None] * inv_freq[None, :]
            freqs = jnp.concatenate([freqs, freqs], axis=-1)
            base = (half_idx + 0.4 * DIM_HEAD) / (1.4 * DIM_HEAD)
            power = (t - n // 2) / float(WINDOW // 2)
            scale = base[None, :] ** power[:, None]
            scale = jnp.concatenate([scale, scale], axis=-1)
            cos, sin = (jnp.cos(freqs), jnp.sin(freqs))
            q = q * cos * scale + rotate_half(q) * sin * scale
            k = k * cos / scale + rotate_half(k) * sin / scale
            return (q, k)

        def local_attention(q, k, v):
            b, h, n, d = q.shape
            w = n // WINDOW
            bq = q.reshape(b, h, w, WINDOW, d) * QK_SCALE
            bk = k.reshape(b, h, w, WINDOW, d)
            bv = v.reshape(b, h, w, WINDOW, d)

            def look_around(t):
                p = jnp.pad(t, ((0, 0), (0, 0), (1, 0), (0, 0), (0, 0)))
                return jnp.concatenate([p[:, :, :w], p[:, :, 1:]], axis=3)
            bk, bv = (look_around(bk), look_around(bv))
            bt = jnp.arange(n).reshape(w, WINDOW)
            btp = jnp.pad(bt, ((1, 0), (0, 0)), constant_values=-1)
            btk = jnp.concatenate([btp[:w], btp[1:]], axis=1)
            sim = jnp.einsum('bhwid,bhwjd->bhwij', bq, bk)
            i = bt[:, :, None]
            j = btk[:, None, :]
            mask = (i < j) | (i > j + WINDOW) | (j == -1)
            sim = jnp.where(mask, -jnp.finfo(sim.dtype).max, sim)
            attn = jax.nn.softmax(sim, axis=-1)
            out = jnp.einsum('bhwij,bhwjd->bhwid', attn, bv)
            return out.reshape(b, h, n, d)

        def _layer(x, wqkv, qs, ksc, wo, lg, lb, w1, b1, w2, b2):
            b, n, _ = x.shape
            h = shift_token(x)
            qkv = h @ wqkv
            q, k, v = jnp.split(qkv, 3, axis=-1)
            to_heads = lambda t: t.reshape(b, n, HEADS, DIM_HEAD).transpose(0, 2, 1, 3)
            q, k, v = (to_heads(q), to_heads(k), to_heads(v))
            q = l2norm(q) * qs
            k = l2norm(k) * ksc
            q, k = rotary_xpos(q, k)
            o = local_attention(q, k, v)
            o = o.transpose(0, 2, 1, 3).reshape(b, n, INNER)
            x = x + o @ wo
            h = shift_token(x)
            mu = h.mean(-1, keepdims=True)
            var = h.var(-1, keepdims=True)
            h = (h - mu) / jnp.sqrt(var + 1e-05) * lg + lb
            h = h @ w1 + b1
            a, g = jnp.split(h, 2, axis=-1)
            h = a * jax.nn.gelu(g, approximate=False)
            x = x + h @ w2 + b2
            return x
        for l in range(DEPTH):
            x = _layer(x, wqkv[l], q_scale[l], k_scale[l], wo[l], ln_g[l], ln_b[l], w1[l], b1[l], w2[l], b2[l])
        return x
    x = x + _L0_xattn_ref(_layernorm(x, axis=-1), ctx_1024, ctx_1024, L0_xattn_Wq_w, L0_xattn_Wq_b, L0_xattn_Wk_w, L0_xattn_Wk_b, L0_xattn_Wv_w, L0_xattn_Wv_b, L0_xattn_Wo_w, L0_xattn_Wo_b)
    x = x + _L0_ffn_ref(_layernorm(x, axis=-1), L0_ffn_wqkv, L0_ffn_q_scale, L0_ffn_k_scale, L0_ffn_wo, L0_ffn_ln_g, L0_ffn_ln_b, L0_ffn_w1, L0_ffn_b1, L0_ffn_w2, L0_ffn_b2)
    return x

_drawn_inputs = setup_inputs


def setup_inputs(seed=0):
    import zlib

    import numpy as np

    out = dict(_drawn_inputs(seed))
    spreads = {'L0_xattn_Wq_b': (0.0, 0.389),
     'L0_xattn_Wk_b': (0.0, 0.8),
     'L0_xattn_Wv_b': (0.0, 0.1),
     'L0_xattn_Wo_b': (0.0, 0.1),
     'L0_ffn_q_scale': (1.0, 0.6),
     'L0_ffn_k_scale': (1.0, 0.6),
     'L0_ffn_ln_g': (1.0, 0.6),
     'L0_ffn_ln_b': (0.0, 0.8),
     'L0_ffn_b1': (0.0, 0.8),
     'L0_ffn_b2': (0.0, 0.1)}
    factors = {}
    for name, (base, spread) in spreads.items():
        noise = np.random.default_rng([zlib.crc32(name.encode()), seed]).standard_normal(out[name].shape)
        drawn = base * np.exp(spread * noise) if base else spread * noise
        out[name] = jnp.asarray(drawn.astype(out[name].dtype))
    for name, factor in factors.items():
        out[name] = (out[name] * factor).astype(out[name].dtype)
    return out
```

```python
import concourse.bass as bass
from concourse import mybir
from concourse.alu_op_type import AluOpType as ALU
from contextlib import ExitStack
import numpy as np

B, S, D = 16, 128, 256
P = 128
C2 = D // P
XH, XD = 16, 16
DEPTH, H, HD = 2, 8, 64
INNER = H * HD
C4 = INNER // P
HID = int(D * 4 * 2 / 3)
MFULL = HID // P
TAIL = HID - MFULL * P
NM = 2 * MFULL + 1
PAIRS = B // 2
QPB = 4
QPP = 2 * QPB
WQKV = C2 * 3 * INNER
WATT = WQKV + C4 * D
W1N = C2 * NM * P
WFFN = W1N + (MFULL + 1) * D
GT = 4
GROUPS = B // GT
SKEW = 2
LN_EPS = 1e-5
NORM_FLOOR2 = 1e-24


class Step:

    def __init__(self, c, j=None):
        self.c, self.j = c, j

    def __add__(self, n):
        return Step(self.c + n, self.j)

    @property
    def slot(self):
        return self.c % 2

    def times(self, k, plus=0):
        return k * self.c + plus if self.j is None else self.j * (2 * k) + (k * self.c + plus)

    def half(self, k, plus=0):
        return k * (self.c // 2) + plus if self.j is None else self.j * k + (k * (self.c // 2) + plus)

    def within(self, lo, hi):
        return self.j is not None or lo <= self.c < hi


class Signals:

    def __init__(self, sem):
        self.consts_loaded = sem("consts_loaded")
        self.x_first_loaded = sem("x_first_loaded")
        self.x_rest_loaded = sem("x_rest_loaded")
        self.wx_loaded = sem("wx_loaded")
        self.watt_loaded = sem("watt_loaded")
        self.wffn_loaded = sem("wffn_loaded")
        self.ctx0_loaded = sem("ctx0_loaded")
        self.ctx1_loaded = sem("ctx1_loaded")
        self.vectors_loaded = sem("vectors_loaded")
        self.y_shifted = sem("y_shifted")
        self.stored = sem("stored")
        self.wait_carried = sem("wait_carried")
        self.ident_bf_made = sem("ident_bf_made")
        self.fills_made = sem("fills_made")
        self.causal_made = sem("causal_made")
        self.rot_scaled_made = sem("rot_scaled_made")
        self.wx_hi_made = sem("wx_hi_made")
        self.wx_lo_made = sem("wx_lo_made")
        self.att_w_hi = sem("att_w_hi")
        self.att_w_made = sem("att_w_made")
        self.ffn_w_hi = sem("ffn_w_hi")
        self.ffn_w_made = sem("ffn_w_made")
        self.b1_product = sem("b1_product")
        self.b1_made = sem("b1_made")
        self.w1_scaled = sem("w1_scaled")
        self.zeros_a = sem("zeros_a")
        self.zeros_made = sem("zeros_made")
        self.qm_zeros_made = sem("qm_zeros_made")
        self.shift_zero = sem("shift_zero")
        self.bn_done = sem("bn_done")
        self.var_ready = sem("var_ready")
        self.eps_added = sem("eps_added")
        self.rstd_ready = sem("rstd_ready")
        self.z_ready = sem("z_ready")
        self.zT_ready = sem("zT_ready")
        self.cT_ready = sem("cT_ready")
        self.zT_hi_ready = sem("zT_hi_ready")
        self.cT_hi_ready = sem("cT_hi_ready")
        self.zT_lo_ready = sem("zT_lo_ready")
        self.cT_lo_ready = sem("cT_lo_ready")
        self.Q_ready = sem("Q_ready")
        self.K_ready = sem("K_ready")
        self.V_ready = sem("V_ready")
        self.q32_ready = sem("q32_ready")
        self.k32_ready = sem("k32_ready")
        self.Q_hi_ready = sem("Q_hi_ready")
        self.K_hi_ready = sem("K_hi_ready")
        self.q_lo_ready = sem("q_lo_ready")
        self.QM_ready = sem("QM_ready")
        self.K_lo_ready = sem("K_lo_ready")
        self.KM_ready = sem("KM_ready")
        self.V_hi_ready = sem("V_hi_ready")
        self.V_lo_ready = sem("V_lo_ready")
        self.xrinv_ready = sem("xrinv_ready")
        self.xO_ready = sem("xO_ready")
        self.xOT_ready = sem("xOT_ready")
        self.xOT_hi_ready = sem("xOT_hi_ready")
        self.xOT_lo_ready = sem("xOT_lo_ready")
        self.xout_ready = sem("xout_ready")
        self.bo_added = sem("bo_added")
        self.x_ready = sem("x_ready")
        self.bn2_done = sem("bn2_done")
        self.var2_ready = sem("var2_ready")
        self.eps2_added = sem("eps2_added")
        self.rstd2_ready = sem("rstd2_ready")
        self.y_ready = sem("y_ready")
        self.xguess_ready = sem("xguess_ready")
        self.xmax_ready = sem("xmax_ready")
        self.xscores_ready = sem("xscores_ready")
        self.xE_ready = sem("xE_ready")
        self.xp1_ready = sem("xp1_ready")
        self.xp2_ready = sem("xp2_ready")
        self.xPV_ready = sem("xPV_ready")
        self.y_tile_ready = sem("y_tile_ready")
        self.yT_ready = sem("yT_ready")
        self.hT_hi_ready = sem("hT_hi_ready")
        self.hT_lo_ready = sem("hT_lo_ready")
        self.q_ready = sem("q_ready")
        self.k_ready = sem("k_ready")
        self.v_ready = sem("v_ready")
        self.squares_ready = sem("squares_ready")
        self.sums_done = sem("sums_done")
        self.ss_ready = sem("ss_ready")
        self.rnorm_ready = sem("rnorm_ready")
        self.qk_ab_ready = sem("qk_ab_ready")
        self.qk_sum = sem("qk_sum")
        self.qk_ready = sem("qk_ready")
        self.v_hi_ready = sem("v_hi_ready")
        self.v_lo_ready = sem("v_lo_ready")
        self.OT_ready = sem("OT_ready")
        self.OT_hi_ready = sem("OT_hi_ready")
        self.OT_lo_ready = sem("OT_lo_ready")
        self.att_out_ready = sem("att_out_ready")
        self.y_att_ready = sem("y_att_ready")
        self.qkT_ready = sem("qkT_ready")
        self.qk_hi_ready = sem("qk_hi_ready")
        self.qk_lo_ready = sem("qk_lo_ready")
        self.qk_bf_ready = sem("qk_bf_ready")
        self.guess_ready = sem("guess_ready")
        self.max_ready = sem("max_ready")
        self.scores_ready = sem("scores_ready")
        self.exp_done = sem("exp_done")
        self.E_ready = sem("E_ready")
        self.p1_ready = sem("p1_ready")
        self.p2_ready = sem("p2_ready")
        self.PV_ready = sem("PV_ready")
        self.rinv_ready = sem("rinv_ready")
        self.O_ready = sem("O_ready")
        self.fbn_done = sem("fbn_done")
        self.fvar_ready = sem("fvar_ready")
        self.feps_added = sem("feps_added")
        self.frstd_ready = sem("frstd_ready")
        self.b2_first = sem("b2_first")
        self.fz_ready = sem("fz_ready")
        self.fzT_ready = sem("fzT_ready")
        self.fzT_hi_ready = sem("fzT_hi_ready")
        self.fzT_lo_ready = sem("fzT_lo_ready")
        self.h_ready = sem("h_ready")
        self.gelu_ready = sem("gelu_ready")
        self.u_ready = sem("u_ready")
        self.u_hi_ready = sem("u_hi_ready")
        self.u_lo_ready = sem("u_lo_ready")
        self.ffn_out_ready = sem("ffn_out_ready")
        self.y_ffn_ready = sem("y_ffn_ready")
        self.b2_added = sem("b2_added")


def wait(engine, semaphore, value):
    if not (isinstance(value, int) and value <= 0):
        engine.wait_ge(semaphore, value)


def wait_apart(engine, semaphore, value, carrier):
    wait(engine, semaphore, value)
    if not isinstance(value, int):
        engine.sem_inc(carrier, 1)


def run_steps(engine, body, first, last, loop_first, loop_last):
    for c in range(first, loop_first):
        body(Step(c))
    assert (loop_last - loop_first + 1) % 2 == 0
    with engine.Fori(0, (loop_last - loop_first + 1) // 2) as j:
        body(Step(loop_first, j))
        body(Step(loop_first + 1, j))
    for c in range(loop_last + 1, last + 1):
        body(Step(c))


def program(nc, x, ctx, wx, bx, bo, watt, scales, rot, wffn, lng, b1, b2, consts, out):
    fp32, f32r, bf16, fp16 = mybir.dt.float32, mybir.dt.float32r, mybir.dt.bfloat16, mybir.dt.float16
    ACT = mybir.ActivationFunctionType
    AX = mybir.AxisListType

    held = ExitStack()

    def sb(name, shape, dt=fp32, at=held):
        return at.enter_context(nc.sbuf_tensor(name, shape, dt))

    def sem(name):
        return held.enter_context(nc.semaphore(name))

    def f(ap):
        return ap.bitcast(fp32)

    x_dram = x.rearrange("b s d -> s b d")
    ctx_dram = ctx.rearrange("b s d -> s b d")
    out_dram = out.rearrange("b s d -> s b d")

    x_all = sb("x_all", [P, B, D])
    y_all = sb("y_all", [P, B, D])
    y_shift = sb("y_shift", [P, B, P])
    att_hi = sb("att_hi", [P, WATT], f32r)
    att_lo = sb("att_lo", [P, WATT], f32r)
    ffn_hi = sb("ffn_hi", [P, WFFN], f32r)
    ffn_lo = sb("ffn_lo", [P, WFFN], f32r)
    stage = sb("stage", [P, WFFN])
    rot_tab = sb("rot_tab", [P, 2, 2, HD])
    rot_scaled = sb("rot_scaled", [P, DEPTH, 2, 2, HD])
    bx_sb = sb("bx_sb", [P, 3, C2])
    bo_sb = sb("bo_sb", [P, D])
    b2_sb = sb("b2_sb", [P, DEPTH, D])
    ln_sb = sb("ln_sb", [P, DEPTH, 2, C2])
    b1_sb = sb("b1_sb", [P, DEPTH, NM])
    const_sb = sb("const_sb", [P, P + 2])
    ident = const_sb[:, 0:P]
    ident_bf = sb("ident_bf", [P, P], bf16)
    neg_half = sb("neg_half", [P, H * 2])
    causal = sb("causal", [P, 4, P], bf16)
    causal32 = sb("causal32", [P, 4, P])
    bn = sb("bn", [P, GT, 2, 6])
    mv = sb("mv", [P, GT, 2])
    rstd = sb("rstd", [P, GT])
    bn2 = sb("bn2", [P, 2, 6])
    mv2 = sb("mv2", [P, 2, 2])
    rstd2 = sb("rstd2", [P, 2])

    held_x = ExitStack()

    def sx(name, shape, dt=fp32):
        return sb(name, shape, dt, held_x)

    Q_hi = [sx(f"Q_hi{i}", [P, C2, 2, P], f32r) for i in range(2)]
    K_hi = [sx(f"K_hi{i}", [P, C2, 2, P], f32r) for i in range(2)]
    K_lo = [sx(f"K_lo{i}", [P, C2, 2, P], f32r) for i in range(2)]
    QM_hi = [sx(f"QM_hi{i}", [P, C2, 2, 2, P], f32r) for i in range(2)]
    QM_lo = [sx(f"QM_lo{i}", [P, C2, 2, 2, P], f32r) for i in range(2)]
    KM_hi = [sx(f"KM_hi{i}", [P, C2, 2, 2, P], f32r) for i in range(2)]
    V_hi = [sx(f"V_hi{i}", [P, 2, XH, XD + 1], fp16) for i in range(2)]
    V_lo = [sx(f"V_lo{i}", [P, 2, XH, XD + 1], fp16) for i in range(2)]
    xOT_hi, xOT_lo = (sx(n, [P, C2, 2, P], f32r) for n in ("xOT_hi", "xOT_lo"))
    x_nm = [sx(f"x_nm{i}", [P, 4], bf16) for i in range(2)]
    x_E = [y_shift[:, 4 * i:4 * i + 4, :] for i in range(4)]
    x_p1 = [sx(f"x_p1{i}", [P, 4, P], fp16) for i in range(4)]
    x_rinv = sx("x_rinv", [P, XH])
    x_O = sx("x_O", [P, 2, D])
    ctx_sb = [sx(f"ctx_sb{i}", [P, 2, D]) for i in range(2)]
    z_sb = sx("z_sb", [P, 2, D])
    zT_hi, zT_lo = (sx(n, [P, C2, 2, P], f32r) for n in ("zT_hi", "zT_lo"))
    cT_hi, cT_lo = (sx(n, [P, C2, 2, P], f32r) for n in ("cT_hi", "cT_lo"))
    q32, k32 = sx("q32", [P, C2, 2, P]), sx("k32", [P, C2, 2, P])
    q_lo = sx("q_lo", [P, C2, 2, P])
    x_p2 = [sx(f"x_p2{i}", [P, 4, P], fp16) for i in range(4)]
    held_x.close()

    held_a = ExitStack()

    def sa(name, shape, dt=fp32):
        return sb(name, shape, dt, held_a)

    y_tile = [sa(f"y_tile{i}", [P, D]) for i in range(2)]
    squares = sa("squares", [P, 2, INNER])
    ss = sa("ss", [P, 2, H])
    rnorm = sa("rnorm", [P, 2, H])
    qk_a = sa("qk_a", [P, 2, INNER])
    qk_b = sa("qk_b", [P, 2, INNER])
    qk = [sa(f"qk{i}", [P, 2, INNER]) for i in range(2)]
    k_hi = [[sa(f"k_hi{i}{h}", [P, 2, P], f32r) for h in range(2)] for i in range(2)]
    k_lo = [[sa(f"k_lo{i}{h}", [P, 2, P], f32r) for h in range(2)] for i in range(2)]
    qm_bf = sa("qm_bf", [P, 2, 2, P], bf16)
    k_bf = sa("k_bf", [P, 2, P], bf16)
    nm = [[sa(f"nm{i}{h}", [P, 4], bf16) for h in range(2)] for i in range(2)]
    E = [sa(f"E{h}", [P, 4, P]) for h in range(2)]
    p1 = [sa(f"p1{h}", [P, 4, P], fp16) for h in range(2)]
    p2 = [sa(f"p2{h}", [P, 4, P], fp16) for h in range(2)]
    rinv = sa("rinv", [P, 2, 4])
    O = sa("O", [P, INNER])
    OT_hi, OT_lo = (sa(n, [P, C4, P], f32r) for n in ("OT_hi", "OT_lo"))
    v_hi = [sa(f"v_hi{i}", [P, H, HD + 1], fp16) for i in range(2)]
    v_lo = [sa(f"v_lo{i}", [P, H, HD + 1], fp16) for i in range(2)]
    hT_hi = [sa(f"hT_hi{i}", [P, 2 * (P + 2)], f32r) for i in range(2)]
    hT_lo = [sa(f"hT_lo{i}", [P, 2 * (P + 2)], f32r) for i in range(2)]
    qm_hi = [[sa(f"qm_hi{i}{h}", [P, 2, 2, P], f32r) for h in range(2)] for i in range(2)]
    qm_lo = [[sa(f"qm_lo{i}{h}", [P, 2, 2, P], f32r) for h in range(2)] for i in range(2)]
    held_a.close()

    held_f = ExitStack()

    def sf(name, shape, dt=fp32):
        return sb(name, shape, dt, held_f)

    z4 = sf("z4", [P, GT, D])
    zf_hi, zf_lo = (sf(n, [P, C2, GT * P], f32r) for n in ("zf_hi", "zf_lo"))
    gel = [sf(f"gel{i}", [P, GT * P]) for i in range(2)]
    u32 = [sf(f"u32{i}", [P, GT * P]) for i in range(2)]
    u_hi, u_lo = (sf(n, [P, MFULL + 1, GT * P], f32r) for n in ("u_hi", "u_lo"))
    held_f.close()

    bank = [held.enter_context(nc.psum_tensor(f"bank{i}", [P, 512], fp32)) for i in range(8)]

    g = Signals(sem)

    block = held.enter_context(nc.Block())

    def wx_part(t, n, c):
        return t[:, (n * C2 + c) * D:(n * C2 + c + 1) * D]

    def wqkv_part(t, c, n):
        return t[:, c * 3 * INNER + n * INNER:c * 3 * INNER + (n + 1) * INNER]

    def wo_part(t, c):
        return t[:, WQKV + c * D:WQKV + (c + 1) * D]

    def w1_part(t, c, m):
        return t[:, (c * NM + m) * P:(c * NM + m + 1) * P]

    def w2_part(t, m):
        return t[:, W1N + m * D:W1N + (m + 1) * D]

    wx_raw = y_all[:, 8:16, :].rearrange("p b d -> p (b d)")

    def hT(t, c):
        return t[:, c * (P + 1):c * (P + 1) + P]

    def hT_out(t):
        return t[:, :].rearrange("p (c n) -> p c n", c=C2)[:, :, 0:P]

    def broadcast(ap, shape):
        return ap.to_broadcast(shape)

    def tiles_of(t, first, n):
        return t[:, bass.ds(first, n), :]

    FIRST = 1
    TILE0 = [l * B for l in range(DEPTH)]
    GRP0 = [l * GROUPS for l in range(DEPTH)]

    @block.sync
    def _(sp):
        sp.dma_start(x_all[:, 0:2, :], x_dram[:, 0:2, :]).then_inc(g.x_first_loaded, 16)
        sp.dma_start(const_sb[:, :], consts).then_inc(g.consts_loaded, 16)
        sp.dma_start(wx_raw, wx).then_inc(g.wx_loaded, 16)
        sp.dma_start(ctx_sb[0][:, :, :], ctx_dram[:, 0:2, :]).then_inc(g.ctx0_loaded, 16)
        for dst, src in ((bx_sb[:, :, :], bx), (bo_sb[:, :], bo.partition_broadcast(P)),
                         (b2_sb[:, :, :], b2.partition_broadcast(P)), (ln_sb[:, :, :, :], lng),
                         (b1_sb[:, :, :], b1), (rot_tab[:, :, :, :], rot),
                         (rot_scaled[:, :, :, :, :], scales.partition_broadcast(P))):
            sp.dma_start(dst, src).then_inc(g.vectors_loaded, 16)
        sp.dma_start(x_all[:, 2:B, :], x_dram[:, 2:B, :]).then_inc(g.x_rest_loaded, 16)
        sp.dma_start(ctx_sb[1][:, :, :], ctx_dram[:, 2:4, :]).then_inc(g.ctx1_loaded, 16)
        sp.dma_start(stage[:, 0:WATT], watt[0]).then_inc(g.watt_loaded, 16)

        with sp.Fori(1, PAIRS // 2) as j:
            for slot in range(2):
                sp.wait_ge(g.cT_ready, j * 2 + (slot - 1))
                sp.dma_start(ctx_sb[slot][:, :, :], ctx_dram[:, bass.ds(j * 4 + 2 * slot, 2), :]
                             ).then_inc((g.ctx0_loaded, g.ctx1_loaded)[slot], 16)

        for l in range(DEPTH):
            sp.wait_ge(g.att_w_made, (l + 1) * PAIRS if l == 0 else PAIRS + GROUPS)
            sp.dma_start(stage[:, 0:WFFN], wffn[l]).then_inc(g.wffn_loaded, 16)
            with sp.Fori(0, B) as t:
                sp.wait_ge(g.y_att_ready, t + (TILE0[l] + 1))
                sp.dma_start(y_shift[1:P, bass.ds(t, 1), :], y_all[0:P - 1, bass.ds(t, 1), P:D]
                             ).then_inc(g.y_shifted, 16)
                wait_apart(sp, g.y_shifted, (t + (TILE0[l] + 1)) * 16, g.wait_carried)
            if l + 1 < DEPTH:
                sp.wait_ge(g.ffn_w_made, (l + 1) * B)
                sp.dma_start(stage[:, 0:WATT], watt[l + 1]).then_inc(g.watt_loaded, 16)
        with sp.Fori(0, GROUPS) as gr:
            sp.wait_ge(g.y_ffn_ready, gr * 2 + (2 * GRP0[DEPTH - 1] + 2 + FIRST))
            sp.dma_start(out_dram[:, bass.ds(gr * GT, GT), :], y_all[:, bass.ds(gr * GT, GT), :]
                         ).then_inc(g.stored, 16)
        sp.wait_ge(g.stored, 16 * GROUPS)

    @block.tensor
    def _(pe):
        def split_product(out_ap, l_hi, l_lo, r_hi, r_lo, first, last):
            nc.tensor.matmul(out_ap, l_hi, r_hi, start=first, stop=False)
            nc.tensor.matmul(out_ap, l_hi, r_lo, start=False, stop=False)
            return nc.tensor.matmul(out_ap, l_lo, r_hi, start=False, stop=last)

        def scores_less_max(out_ap, k_h, k_l, q_h, q_l, less):
            nc.tensor.matmul(out_ap, k_h, q_h, start=True, stop=False)
            for e in range(2):
                nc.tensor.matmul(out_ap[:, e, :], broadcast(less[:, e:e + 1], [P, P]), ident_bf[:, :],
                                 start=False, stop=False, skip_group_check=True)
            nc.tensor.matmul(out_ap, k_h, q_l, start=False, stop=False)
            return nc.tensor.matmul(out_ap, k_l, q_h, start=False, stop=True)

        def project_z(h):
            pe.wait_ge(g.z_ready, h.times(1, 1))
            if h.j is None:
                wait(pe, g.k32_ready, h.c)
            wait(pe, g.x_ready, h.times(1, -2))
            v = bank[0][:, :].rearrange("p (c b t) -> p c b t", c=C2, b=2)
            for b in range(2):
                for c in range(C2):
                    last = nc.tensor.transpose(v[:, c, b, :], z_sb[:, b, c * P:(c + 1) * P], ident)
            last.then_inc(g.zT_ready, 1)
            pe.wait_ge((g.ctx0_loaded, g.ctx1_loaded)[h.slot], h.half(16, 16))
            wait(pe, g.V_lo_ready, h.times(1))
            v = bank[1][:, :].rearrange("p (c b t) -> p c b t", c=C2, b=2)
            for b in range(2):
                for c in range(C2):
                    last = nc.tensor.transpose(v[:, c, b, :], ctx_sb[h.slot][:, b, c * P:(c + 1) * P], ident)
            last.then_inc(g.cT_ready, 1)

        def project_qk(h, n, to, t_hi, t_lo):
            v = bank[to][:, :].rearrange("p (o n) -> p o n", o=C2)
            for o in range(C2):
                for c in range(C2):
                    last = split_product(
                        v[:, o, :], wx_part(ffn_hi, n, c)[:, o * P:(o + 1) * P], wx_part(ffn_lo, n, c)[:, o * P:(o + 1) * P],
                        t_hi[:, c, :, :], t_lo[:, c, :, :], c == 0, c == C2 - 1)
            return last

        def project_q(h):
            if h.j is None and h.c == 0:
                pe.wait_ge(g.wx_lo_made, 4)
            pe.wait_ge(g.zT_lo_ready, h.times(1, 1))
            if h.j is None:
                wait(pe, g.q32_ready, h.c)
            wait(pe, g.xOT_lo_ready, h.times(1, -2))
            project_qk(h, 0, 2, zT_hi, zT_lo).then_inc(g.Q_ready, 1)

        def project_k(h):
            pe.wait_ge(g.cT_lo_ready, h.times(1, 1))
            pe.wait_ge(g.zT_lo_ready, h.times(1, 1))
            project_qk(h, 1, 0, cT_hi, cT_lo).then_inc(g.K_ready, 1)

        def project_v(h):
            pe.wait_ge(g.cT_lo_ready, h.times(1, 1))
            v = bank[1][:, :].rearrange("p (b n) -> p b n", b=2)
            for b in range(2):
                for c in range(C2):
                    last = split_product(v[:, b, :], cT_hi[:, c, b, :], cT_lo[:, c, b, :],
                                         wx_part(ffn_hi, 2, c), wx_part(ffn_lo, 2, c), c == 0, c == C2 - 1)
            last.then_inc(g.V_ready, 1)

        def x_guess(p, q):
            b, r, n = q // QPB, q % QPB, q % 2
            if q == 0:
                pe.wait_ge(g.Q_hi_ready, p.times(1, 1))
                pe.wait_ge(g.KM_ready, p.times(1, 1))
            v = bank[3 + n][:, :].rearrange("p (c n) -> p c n", c=C2)
            rows = slice(32 * r, 32 * r + 32)
            for c in range(C2):
                last = nc.tensor.matmul(v[:, c, :], Q_hi[p.slot][rows, c, b, :],
                                        KM_hi[p.slot][rows, c, b, :, :], start=True, stop=True)
            last.then_inc(g.xguess_ready, 1)

        def x_scores(p, q):
            b, r, n = q // QPB, q % QPB, q % 2
            if q == 0:
                pe.wait_ge(g.QM_ready, p.times(1, 1))
                pe.wait_ge(g.K_lo_ready, p.times(1, 1))
            pe.wait_ge(g.xmax_ready, p.times(QPP, q + 1))
            wait(pe, g.xE_ready, p.times(QPP, q - 1))
            v = bank[5 + n][:, :].rearrange("p (c e n) -> p c e n", c=C2, e=2)
            rows = slice(32 * r, 32 * r + 32)
            for c in range(C2):
                last = scores_less_max(
                    v[:, c, :, :], K_hi[p.slot][rows, c, b, :], K_lo[p.slot][rows, c, b, :],
                    QM_hi[p.slot][rows, c, b, :, :], QM_lo[p.slot][rows, c, b, :, :], x_nm[n][:, 2 * c:2 * c + 2])
            last.then_inc(g.xscores_ready, 1)

        def x_weighted(p, q):
            b, r, n = q // QPB, q % QPB, q % 4
            if q == 0:
                pe.wait_ge(g.V_lo_ready, p.times(1, 1))
            if r == 0:
                wait(pe, g.xO_ready, p.times(2, b))
            pe.wait_ge(g.xp2_ready, p.times(QPP, q + 1))
            v = bank[7][:, 0:XH * (XD + 1)].rearrange("p (h n) -> p h n", h=XH)
            for c in range(C2):
                for e in range(2):
                    h, i = c * 8 + 2 * r + e, 2 * c + e
                    nc.tensor.matmul(v[:, h, :], x_p1[n][:, i, :], V_hi[p.slot][:, b, h, :], start=True, stop=False)
                    nc.tensor.matmul(v[:, h, :], x_p1[n][:, i, :], V_lo[p.slot][:, b, h, :], start=False, stop=False)
                    last = nc.tensor.matmul(v[:, h, :], x_p2[n][:, i, :], V_hi[p.slot][:, b, h, :], start=False, stop=True)
            last.then_inc(g.xPV_ready, 1)

        def x_transpose_o(t, h):
            pe.wait_ge(g.xO_ready, t.times(2, 2))
            if h is not None:
                pe.wait_ge(g.q32_ready, h.times(1, 1))
            else:
                wait(pe, g.xOT_lo_ready, t.times(1))
            v = bank[2][:, :].rearrange("p (c b t) -> p c b t", c=C2, b=2)
            for b in range(2):
                for c in range(C2):
                    last = nc.tensor.transpose(v[:, c, b, :], x_O[:, b, c * P:(c + 1) * P], ident)
            last.then_inc(g.xOT_ready, 1)

        def x_output(t, h):
            pe.wait_ge(g.xOT_lo_ready, t.times(1, 1))
            if h is not None:
                pe.wait_ge(g.k32_ready, h.times(1, 1))
            else:
                wait(pe, g.x_ready, t.times(1))
            v = bank[0][:, :].rearrange("p (b n) -> p b n", b=2)
            for b in range(2):
                for c in range(C2):
                    last = split_product(v[:, b, :], xOT_hi[:, c, b, :], xOT_lo[:, c, b, :],
                                         wx_part(ffn_hi, 3, c), wx_part(ffn_lo, 3, c), c == 0, c == C2 - 1)
            last.then_inc(g.xout_ready, 1)

        pe.wait_ge(g.consts_loaded, 16)
        pe.wait_ge(g.ident_bf_made, 1)
        pe.wait_ge(g.fills_made, 1)

        def x_step(p):
            head, tail = p + 1, p + (-1)
            heads, tails = head.within(0, PAIRS), tail.within(0, PAIRS)
            here = p.within(0, PAIRS)
            hh = head if heads else None
            for q in range(QPP):
                if q < 2 and tails:
                    x_weighted(tail, QPP - 2 + q)
                if q in (3, 4, 5, 7) and here:
                    x_weighted(p, q - 2)
                if q < QPP - 1 and here:
                    x_guess(p, q + 1)
                if q == QPP - 1 and heads:
                    x_guess(head, 0)
                if here:
                    x_scores(p, q)
                if heads:
                    if q == 0:
                        project_z(head)
                    if q == 2:
                        project_q(head)
                    if q == 3:
                        project_k(head)
                    if q == 5:
                        project_v(head)
                if tails:
                    if q == 4:
                        x_transpose_o(tail, hh)
                    if q == 6:
                        x_output(tail, hh)
                if q in (2, 6) and here:
                    x_weighted(p, q - 2)

        run_steps(pe, x_step, -1, PAIRS, 2, PAIRS - 3)

        def att_transpose_y(a, t0):
            pe.wait_ge(g.y_tile_ready, a.times(1, t0 + 1))
            if a.within(0, 1) and a.j is None:
                wait(pe, g.y_ffn_ready, t0 // B * 2 * GROUPS + FIRST)
                wait(pe, g.x_ready, PAIRS)
            if a.j is None:
                wait(pe, g.hT_lo_ready, t0 + a.c)
            wait(pe, g.y_att_ready, a.times(1, t0 - 1 - SKEW))
            for c in range(C2):
                last = nc.tensor.transpose(bank[7][:, c * P:(c + 1) * P], y_tile[a.slot][:, c * P:(c + 1) * P], ident)
            last.then_inc(g.yT_ready, 1)

        def project(a, n):
            for c in range(C2):
                last = split_product(bank[n][:, :], hT(hT_hi[a.slot], c), hT(hT_lo[a.slot], c),
                                     wqkv_part(att_hi, c, n), wqkv_part(att_lo, c, n), c == 0, c == C2 - 1)
            return last

        def att_qk(a, t0, n):
            if n == 0:
                pe.wait_ge(g.hT_lo_ready, a.times(1, t0 + 1))
                if a.j is None and a.c == 0:
                    pe.wait_ge(g.att_w_made, PAIRS if t0 == 0 else PAIRS + GROUPS)
            wait(pe, g.qk_ab_ready, a.times(2, 2 * t0 + n - 1))
            project(a, n).then_inc((g.q_ready, g.k_ready)[n], 1)

        def att_v(b, t0):
            wait(pe, g.v_lo_ready, b.times(1, t0))
            project(b, 2).then_inc(g.v_ready, 1)

        def att_transpose_qk(t, t0, h):
            if h == 0:
                pe.wait_ge(g.qk_ready, t.times(2, 2 * t0 + 2))
            if h == 1:
                pe.wait_ge(g.qk_lo_ready, t.times(2, 2 * t0 + h))
            v = bank[3][:, :].rearrange("p (n j t) -> p n j t", n=2, j=2)
            for n in range(2):
                for j in range(2):
                    cols = slice((2 * h + j) * P, (2 * h + j + 1) * P)
                    last = nc.tensor.transpose(v[:, n, j, :], qk[t.slot][:, n, cols], ident)
            last.then_inc(g.qkT_ready, 1)

        def att_guess(t, t0, h):
            pe.wait_ge(g.qk_bf_ready, t.times(2, 2 * t0 + h + 1))
            v = bank[4][:, :].rearrange("p (j e t) -> p j e t", j=2, e=2)
            for j in range(2):
                for e in range(2):
                    nc.tensor.matmul(v[:, j, e, :], qm_bf[:, j, e, :], k_bf[:, j, :], start=(j, e) == (0, 0), stop=False,
                                     skip_group_check=True)
            last = nc.tensor.matmul(bank[4][:, :], ident_bf[:, :], causal[:, :, :], start=False, stop=True,
                                    skip_group_check=True)
            last.then_inc(g.guess_ready, 1)

        def att_scores(t, t0, h):
            pe.wait_ge(g.qk_lo_ready, t.times(2, 2 * t0 + h + 1))
            pe.wait_ge(g.max_ready, t.times(2, 2 * t0 + h + 1))
            wait(pe, g.exp_done, t.times(2, 2 * t0 + h))
            v = bank[5][:, :].rearrange("p (j e t) -> p j e t", j=2, e=2)
            kh, kl, qh, ql = (x[t.slot][h] for x in (k_hi, k_lo, qm_hi, qm_lo))
            for j in range(2):
                last = scores_less_max(v[:, j, :, :], kh[:, j, :], kl[:, j, :], qh[:, j, :, :], ql[:, j, :, :],
                                       nm[t.slot][h][:, 2 * j:2 * j + 2])
            last.then_inc(g.scores_ready, 1)

        def att_weighted(t, t0, h):
            if h == 0:
                pe.wait_ge(g.v_lo_ready, t.times(1, t0 + 1))
            pe.wait_ge(g.p2_ready, t.times(2, 2 * t0 + h + 1))
            wait(pe, g.O_ready, t.times(2, 2 * t0 + h))
            v = bank[6][:, 0:4 * (HD + 1)].rearrange("p (h n) -> p h n", h=4)
            for i in range(4):
                vh, vl = v_hi[t.slot][:, 4 * h + i, :], v_lo[t.slot][:, 4 * h + i, :]
                nc.tensor.matmul(v[:, i, :], p1[h][:, i, :], vh, start=True, stop=False)
                nc.tensor.matmul(v[:, i, :], p1[h][:, i, :], vl, start=False, stop=False)
                last = nc.tensor.matmul(v[:, i, :], p2[h][:, i, :], vh, start=False, stop=True)
            last.then_inc(g.PV_ready, 1)

        def att_transpose_o(t, t0):
            pe.wait_ge(g.O_ready, t.times(2, 2 * t0 + 2))
            if (t + (1 + SKEW)).within(0, B):
                pe.wait_ge(g.hT_lo_ready, t.times(1, t0 + 4))
            else:
                wait(pe, g.y_att_ready, t.times(1, t0))
            for c in range(C4):
                last = nc.tensor.transpose(bank[7][:, c * P:(c + 1) * P], O[:, c * P:(c + 1) * P], ident)
            last.then_inc(g.OT_ready, 1)

        def att_output(t, t0, part):
            if part == 0:
                pe.wait_ge(g.OT_lo_ready, t.times(1, t0 + 1))
            for c in (2 * part, 2 * part + 1):
                last = split_product(bank[7][:, 0:D], OT_hi[:, c, :], OT_lo[:, c, :],
                                     wo_part(att_hi, c), wo_part(att_lo, c), c == 0, c == C4 - 1)
            if part == 1:
                last.then_inc(g.att_out_ready, 1)

        def att_step(t0):
            def body(i):
                a, b, c, d = i + 2, i + 1, i, i + (-1)
                on = lambda t: t.within(0, B)
                if on(c):
                    att_scores(c, t0, 0)
                if on(a):
                    att_transpose_y(a, t0)
                if on(d):
                    att_weighted(d, t0, 1)
                if on(b):
                    att_v(b, t0)
                if on(c):
                    att_guess(c, t0, 1)
                if on(a):
                    att_qk(a, t0, 0)
                if on(d):
                    att_transpose_o(d, t0)
                if on(a):
                    att_qk(a, t0, 1)
                if on(b):
                    att_transpose_qk(b, t0, 0)
                if on(c):
                    att_scores(c, t0, 1)
                    att_weighted(c, t0, 0)
                if on(d):
                    att_output(d, t0, 0)
                if on(b):
                    att_guess(b, t0, 0)
                    att_transpose_qk(b, t0, 1)
                if on(d):
                    att_output(d, t0, 1)
            return body

        def b1_product(l):
            pe.wait_ge(g.wffn_loaded, 16 * (l + 1))
            pe.wait_ge(g.vectors_loaded, 7 * 16)
            if l > 0:
                pe.wait_ge(g.O_ready, 2 * TILE0[l])
            for m in range(NM):
                for c in range(C2):
                    last = nc.tensor.matmul(bank[6][:, m:m + 1], w1_part(stage, c, m), ln_sb[:, l, 1, c:c + 1],
                                            start=c == 0, stop=c == C2 - 1)
            last.then_inc(g.b1_product, 1)

        def ffn_transpose(gr):
            pe.wait_ge(g.fz_ready, gr + 1)
            wait(pe, g.fzT_lo_ready, gr * 2)
            for c in range(C2):
                for t in range(GT):
                    last = nc.tensor.transpose(bank[c][:, t * P:(t + 1) * P], z4[:, t, c * P:(c + 1) * P], ident)
                last.then_inc(g.fzT_ready, 1)

        def ffn_up(gr, m):
            a = 2 + 2 * (m % 2)
            if m == 0:
                pe.wait_ge(g.fzT_lo_ready, gr * 2 + 2)
            if m >= 2:
                pe.wait_ge(g.u_ready, gr * (MFULL + 1) + (m - 1))
            for k in range(2 if m < MFULL else 1):
                for c in range(C2):
                    w = [w1_part(t, c, 2 * m + k) for t in (ffn_hi, ffn_lo)]
                    last = split_product(bank[a + k][:, :], w[0], w[1], zf_hi[:, c, :], zf_lo[:, c, :], c == 0, c == C2 - 1)
            last.then_inc(g.h_ready, 1)

        def ffn_down(gr):
            wait(pe, g.y_ffn_ready, gr * 2 + FIRST)
            for i in range(2):
                for t in range(2):
                    for m in range(MFULL + 1):
                        if (i, t) == (0, 0):
                            pe.wait_ge(g.u_lo_ready, gr * (MFULL + 1) + (m + 1))
                        rows = slice(0, P if m < MFULL else 64)
                        cols = slice((2 * i + t) * P, (2 * i + t + 1) * P)
                        last = split_product(bank[6 + i][:, t * D:(t + 1) * D], u_hi[rows, m, cols], u_lo[rows, m, cols],
                                             w2_part(ffn_hi, m)[rows, :], w2_part(ffn_lo, m)[rows, :], m == 0, m == MFULL)
                last.then_inc(g.ffn_out_ready, 1)

        for l in range(DEPTH):
            t0, g0 = TILE0[l], GRP0[l]
            step = att_step(t0)
            step(Step(-SKEW))
            step(Step(-1))
            b1_product(l)
            pe.wait_ge(g.b1_made, l + 1)
            run_steps(pe, step, 0, B, 2, B - 5)
            pe.wait_ge(g.ffn_w_made, B * (l + 1))
            pe.wait_ge(g.y_att_ready, t0 + B)
            ffn_transpose(g0)
            with pe.Fori(0, GROUPS - 1) as j:
                for m in range(MFULL + 1):
                    ffn_up(j + g0, m)
                ffn_transpose(j + (g0 + 1))
                ffn_down(j + g0)
            for m in range(MFULL + 1):
                ffn_up(g0 + GROUPS - 1, m)
            ffn_down(g0 + GROUPS - 1)

    @block.scalar
    def _(act):
        def copy(o, i):
            return nc.scalar.activation(o, i, ACT.Copy)

        act.wait_ge(g.wx_loaded, 16)
        for n in range(4):
            cols = slice(n * 2 * D, (n + 1) * 2 * D)
            copy(ffn_hi[:, cols], wx_raw[:, cols]).then_inc(g.wx_hi_made, 1)
        act.wait_ge(g.vectors_loaded, 7 * 16)

        def x_exp(p, q):
            n = q % 4
            act.wait_ge(g.xscores_ready, p.times(QPP, q + 1))
            wait(act, g.xp2_ready, p.times(QPP, q - 3))
            nc.scalar.activation(x_E[n].rearrange("p i t -> p (i t)"), bank[5 + q % 2][:, :], ACT.Exp,
                                 scale=float(XD) ** -0.5).then_inc(g.xE_ready, 1)
            act.wait_ge(g.xE_ready, p.times(QPP, q + 1))
            wait(act, g.xPV_ready, p.times(QPP, q - 3))
            copy(x_p1[n][:, :, :], x_E[n]).then_inc(g.xp1_ready, 1)

        def x_step(p):
            head, tail = p + 1, p + (-1)
            heads, tails, here = head.within(0, PAIRS), tail.within(0, PAIRS), p.within(0, PAIRS)
            for q in range(QPP):
                if heads and q == 1:
                    act.wait_ge(g.zT_ready, head.times(1, 1))
                    wait(act, g.Q_ready, head.times(1))
                    copy(zT_hi[:, :, :, :].rearrange("p c b t -> p (c b t)"), bank[0][:, :]).then_inc(g.zT_hi_ready, 1)
                    act.wait_ge(g.cT_ready, head.times(1, 1))
                    wait(act, g.V_ready, head.times(1))
                    copy(cT_hi[:, :, :, :].rearrange("p c b t -> p (c b t)"), bank[1][:, :]).then_inc(g.cT_hi_ready, 1)
                if heads and q in (3, 4):
                    n = q - 3
                    act.wait_ge((g.Q_ready, g.K_ready)[n], head.times(1, 1))
                    if n == 0:
                        wait(act, g.q_lo_ready, head.times(1))
                    else:
                        wait(act, g.K_lo_ready, head.times(1))
                    for c in range(C2):
                        last = nc.scalar.activation((q32, k32)[n][:, c, :, :].rearrange("p b t -> p (b t)"),
                                                    bank[(2, 0)[n]][:, c * D:(c + 1) * D], ACT.Identity,
                                                    bias=bx_sb[:, n, c:c + 1])
                    last.then_inc((g.q32_ready, g.k32_ready)[n], 1)
                if tails and q == 5:
                    act.wait_ge(g.xOT_ready, tail.times(1, 1))
                    wait(act, g.xout_ready, tail.times(1))
                    for c in range(C2):
                        last = nc.scalar.activation(xOT_hi[:, c, :, :].rearrange("p b t -> p (b t)"),
                                                    bank[2][:, c * D:(c + 1) * D], ACT.Identity, bias=bx_sb[:, 2, c:c + 1])
                    last.then_inc(g.xOT_hi_ready, 1)
                if heads and q == 6:
                    act.wait_ge(g.V_ready, head.times(1, 1))
                    wait(act, g.xPV_ready, head.times(QPP, -QPP))
                    copy(V_hi[head.slot][:, :, :, 0:XD].rearrange("p b h n -> p (b h) n"),
                         bank[1][:, :].rearrange("p (h n) -> p h n", n=XD)).then_inc(g.V_hi_ready, 1)
                if here:
                    x_exp(p, q)

        run_steps(act, x_step, -1, PAIRS, 2, PAIRS - 3)

        def y_copy(a, t0):
            wait_apart(act, g.yT_ready, a.times(1, t0 - 1), g.wait_carried)
            copy(y_tile[a.slot][:, :], y_all[:, bass.ds(a.times(1), 1), :].squeeze(1)).then_inc(g.y_tile_ready, 1)

        def att_hT(a, t0):
            act.wait_ge(g.yT_ready, a.times(1, t0 + 1))
            wait(act, g.v_ready, a.times(1, t0 - 1))
            copy(hT_out(hT_hi[a.slot]), bank[7][:, 0:D].rearrange("p (c t) -> p c t", c=C2)).then_inc(g.hT_hi_ready, 1)

        def att_squares(a, t0, n):
            act.wait_ge((g.q_ready, g.k_ready)[n], a.times(1, t0 + 1))
            wait(act, g.sums_done, a.times(2, 2 * t0 + n - 1))
            nc.scalar.activation(squares[:, n, :], bank[n][:, :], ACT.Square).then_inc(g.squares_ready, 1)

        def att_v(a, t0):
            act.wait_ge(g.v_ready, a.times(1, t0 + 1))
            wait(act, g.PV_ready, a.times(2, 2 * t0 - 2))
            copy(v_hi[a.slot][:, :, 0:HD], bank[2][:, :].rearrange("p (h n) -> p h n", h=H)).then_inc(g.v_hi_ready, 1)

        def att_qk_hi(t, t0, h):
            act.wait_ge(g.qkT_ready, t.times(2, 2 * t0 + h + 1))
            wait(act, g.scores_ready, t.times(2, 2 * t0 + h - 3))
            v = bank[3][:, :].rearrange("p (n j t) -> p n j t", n=2, j=2)
            for e in range(2):
                rows = slice(64 * e, 64 * e + 64)
                copy(qm_hi[t.slot][h][rows, :, e, :], v[rows, 0, :, :])
            copy(k_hi[t.slot][h][:, :, :], v[:, 1, :, :]).then_inc(g.qk_hi_ready, 1)

        def att_qk_bf(t, t0, h):
            wait(act, g.guess_ready, t.times(2, 2 * t0 + h))
            act.wait_ge(g.qk_hi_ready, t.times(2, 2 * t0 + h + 1))
            copy(qm_bf[:, :, :, :], f(qm_hi[t.slot][h][:, :, :, :]))
            copy(k_bf[:, :, :], f(k_hi[t.slot][h][:, :, :])).then_inc(g.qk_bf_ready, 1)

        def att_exp(t, t0, h):
            act.wait_ge(g.scores_ready, t.times(2, 2 * t0 + h + 1))
            wait(act, g.p2_ready, t.times(2, 2 * t0 + h - 1))
            nc.scalar.activation(E[h][:, :, :].rearrange("p i t -> p (i t)"), bank[5][:, :], ACT.Exp).then_inc(g.exp_done, 1)

        def att_p1(t, t0, h):
            act.wait_ge(g.E_ready, t.times(2, 2 * t0 + h + 1))
            wait(act, g.PV_ready, t.times(2, 2 * t0 + h - 1))
            copy(p1[h][:, :, :], E[h][:, :, :]).then_inc(g.p1_ready, 1)

        def att_oT(t, t0):
            act.wait_ge(g.OT_ready, t.times(1, t0 + 1))
            wait(act, g.att_out_ready, t.times(1, t0))
            copy(OT_hi[:, :, :].rearrange("p c t -> p (c t)"), bank[7][:, :]).then_inc(g.OT_hi_ready, 1)

        def weights_high(d, t0):
            n = WFFN // B
            copy(ffn_hi[:, bass.ds(d.times(n), n)], stage[:, bass.ds(d.times(n), n)]).then_inc(g.ffn_w_hi, 1)

        def att_step(t0):
            def body(i):
                a, b, c, d = i + 2, i + 1, i, i + (-1)
                on = lambda t: t.within(0, B)
                if on(c):
                    att_qk_hi(c, t0, 1)
                    att_qk_bf(c, t0, 1)
                    att_exp(c, t0, 0)
                if on(a):
                    att_hT(a, t0)
                if on(a + 1):
                    y_copy(a + 1, t0)
                if on(d):
                    weights_high(d, t0)
                if on(c):
                    att_p1(c, t0, 0)
                if on(b):
                    att_v(b, t0)
                if on(a):
                    att_squares(a, t0, 0)
                if on(d):
                    att_oT(d, t0)
                if on(a):
                    att_squares(a, t0, 1)
                if on(b):
                    att_qk_hi(b, t0, 0)
                    att_qk_bf(b, t0, 0)
                if on(c):
                    att_exp(c, t0, 1)
                if on(c):
                    att_p1(c, t0, 1)
            return body

        def ffn_hT(gr):
            for c in range(C2):
                act.wait_ge(g.fzT_ready, gr * 2 + (c + 1))
                if c == 0:
                    wait(act, g.h_ready, gr * (MFULL + 1))
                copy(zf_hi[:, c, :], bank[c][:, :]).then_inc(g.fzT_hi_ready, 1)

        def ffn_gelu(gr, m, l):
            act.wait_ge(g.h_ready, gr * (MFULL + 1) + (m + 1))
            if m >= 2:
                act.wait_ge(g.u_ready, gr * (MFULL + 1) + (m - 1))
            a = 2 + 2 * (m % 2)
            if m < MFULL:
                src, dst, bias = bank[a + 1][:, :], gel[m % 2][:, :], b1_sb[:, l, 2 * m + 1:2 * m + 2]
            else:
                src, dst, bias = bank[a][64:P, :], gel[m % 2][0:64, :], b1_sb[64:P, l, 2 * m:2 * m + 1]
            nc.scalar.activation(dst, src, ACT.Gelu, bias=bias).then_inc(g.gelu_ready, 1)

        def ffn_u_hi(gr, m):
            act.wait_ge(g.u_ready, gr * (MFULL + 1) + (m + 1))
            if m == 0:
                wait(act, g.ffn_out_ready, gr * 2 + FIRST)
            rows = slice(0, P if m < MFULL else 64)
            copy(u_hi[rows, m, :], u32[m % 2][rows, :]).then_inc(g.u_hi_ready, 1)

        def ffn_group(gr, l):
            for m in range(MFULL + 1):
                ffn_gelu(gr, m, l)
                if m > 0:
                    ffn_u_hi(gr, m - 1)
            ffn_u_hi(gr, MFULL)

        for l in range(DEPTH):
            t0, g0 = TILE0[l], GRP0[l]
            if l == 0:
                act.wait_ge(g.zeros_made, 1)
                act.wait_ge(g.qm_zeros_made, 1)
            act.wait_ge(*((g.y_ready, PAIRS) if l == 0 else (g.y_ffn_ready, 2 * GRP0[l] + FIRST)))
            y_copy(Step(0), t0)
            step = att_step(t0)
            for c in range(-SKEW, 1):
                step(Step(c))
            act.wait_ge(g.w1_scaled, l + 1)
            run_steps(act, step, 1, B, 2, B - 5)
            act.wait_ge(g.y_att_ready, t0 + B)
            act.wait_ge(g.b1_made, l + 1)
            ffn_hT(g0)
            with act.Fori(0, GROUPS - 1) as j:
                ffn_group(j + g0, l)
                ffn_hT(j + (g0 + 1))
            ffn_group(g0 + GROUPS - 1, l)

    @block.vector
    def _(dve):
        def copy(o, i):
            return nc.vector.tensor_copy(o, i)

        def sub(o, a, b):
            return nc.vector.tensor_tensor(o, a, b, ALU.subtract)

        dve.wait_ge(g.consts_loaded, 16)
        copy(ident_bf[:, :], ident).then_inc(g.ident_bf_made, 1)
        for i in range(2):
            nc.vector.memset(V_hi[i][:, :, :, XD:XD + 1], 1.0).then_inc((g.y_ffn_ready, g.ffn_out_ready)[i], FIRST)
            last = nc.vector.memset(V_lo[i][:, :, :, XD:XD + 1], 0.0)
        last.then_inc(g.fills_made, 1)
        dve.wait_ge(g.causal_made, 2)
        copy(causal[:, :, :], causal32[:, :, :]).then_inc(g.causal_made, 1)

        def ln_stats(h):
            if h.j is None and h.c < 2:
                dve.wait_ge((g.x_first_loaded, g.x_rest_loaded)[h.c], 16)
            wait_apart(dve, g.z_ready, h.times(1), g.wait_carried)
            for b in range(2):
                last = nc.vector.bn_stats(bn[:, b, 0, :], x_all[:, bass.ds(h.times(2, b), 1), :].squeeze(1))
            last.then_inc(g.bn_done, 1)
            wait_apart(dve, g.bn_done, h.times(1, 1), g.wait_carried)
            for b in range(2):
                last = nc.vector.bn_aggr(mv[:, b, :], bn[:, b, 0, :])
            last.then_inc(g.var_ready, 1)

        def ln_apply(h):
            dve.wait_ge(g.rstd_ready, h.times(1, 1))
            wait(dve, g.zT_ready, h.times(1))
            for b in range(2):
                last = nc.vector.tensor_scalar(z_sb[:, b, :], x_all[:, bass.ds(h.times(2, b), 1), :].squeeze(1),
                                               mv[:, b, 0:1], rstd[:, b:b + 1], ALU.subtract, ALU.mult)
            last.then_inc(g.z_ready, 1)

        def flat(t):
            return t[:, :, :, :].rearrange("p c b t -> p (c b t)")

        def x_low(h, lo, hi, src, ready_hi, ready_lo, used):
            dve.wait_ge(ready_hi, h.times(1, 1))
            wait(dve, used, h.times(1))
            sub(flat(lo), src, f(flat(hi))).then_inc(ready_lo, 1)

        def x_max(p, q):
            n = q % 2
            dve.wait_ge(g.xguess_ready, p.times(QPP, q + 1))
            wait(dve, g.xscores_ready, p.times(QPP, q - 1))
            nc.vector.tensor_reduce(x_nm[n][:, :], bank[3 + n][:, :].rearrange("p (i t) -> p i t", i=4), AX.X,
                                    ALU.max, negate=True).then_inc(g.xmax_ready, 1)

        def x_p2_part(p, q):
            n = q % 4
            dve.wait_ge(g.xp1_ready, p.times(QPP, q + 1))
            wait(dve, g.xPV_ready, p.times(QPP, q - 3))
            sub(x_p2[n][:, :, :], x_E[n], x_p1[n][:, :, :]).then_inc(g.xp2_ready, 1)

        def x_normalise(p, b):
            dve.wait_ge(g.xPV_ready, p.times(QPP, QPB * (b + 1)))
            v = bank[7][:, 0:XH * (XD + 1)].rearrange("p (h n) -> p h n", h=XH)
            wait(dve, g.xO_ready, p.times(2, b))
            nc.vector.reciprocal(x_rinv[:, :], v[:, :, XD:XD + 1].squeeze(2)).then_inc(g.xrinv_ready, 1)
            dve.wait_ge(g.xrinv_ready, p.times(2, b + 1))
            wait(dve, g.xOT_ready, p.times(1))
            nc.vector.tensor_tensor(x_O[:, b, :].rearrange("p (h n) -> p h n", h=XH), v[:, :, 0:XD],
                                    broadcast(x_rinv[:, :].unsqueeze(2), [P, XH, XD]), ALU.mult).then_inc(g.xO_ready, 1)

        def x_oT_low(t):
            dve.wait_ge(g.xOT_hi_ready, t.times(1, 1))
            wait(dve, g.xout_ready, t.times(1))
            for c in range(C2):
                last = nc.vector.scalar_tensor_tensor(
                    xOT_lo[:, c, :, :].rearrange("p b t -> p (b t)"), bank[2][:, c * D:(c + 1) * D], bx_sb[:, 2, c:c + 1],
                    f(xOT_hi[:, c, :, :]).rearrange("p b t -> p (b t)"), ALU.add, ALU.subtract)
            last.then_inc(g.xOT_lo_ready, 1)

        def x_residual(t):
            dve.wait_ge(g.xout_ready, t.times(1, 1))
            dve.wait_ge(g.bo_added, t.times(1, 1))
            pair = tiles_of(x_all, t.times(2), 2)
            nc.vector.tensor_tensor(pair, bank[0][:, :].rearrange("p (b n) -> p b n", b=2), pair,
                                    ALU.add).then_inc(g.x_ready, 1)
            dve.wait_ge(g.x_ready, t.times(1, 1))
            wait_apart(dve, g.y_ready, t.times(1), g.wait_carried)
            for b in range(2):
                last = nc.vector.bn_stats(bn2[:, b, :], x_all[:, bass.ds(t.times(2, b), 1), :].squeeze(1))
            last.then_inc(g.bn2_done, 1)
            wait_apart(dve, g.bn2_done, t.times(1, 1), g.wait_carried)
            for b in range(2):
                last = nc.vector.bn_aggr(mv2[:, b, :], bn2[:, b, :])
            last.then_inc(g.var2_ready, 1)

        def y_first(t):
            dve.wait_ge(g.rstd2_ready, t.times(1, 1))
            for b in range(2):
                last = nc.vector.tensor_scalar(y_all[:, bass.ds(t.times(2, b), 1), :].squeeze(1),
                                               x_all[:, bass.ds(t.times(2, b), 1), :].squeeze(1),
                                               mv2[:, b, 0:1], rstd2[:, b:b + 1], ALU.subtract, ALU.mult)
            last.then_inc(g.y_ready, 1)

        ln_stats(Step(0))
        ln_apply(Step(0))
        for n in range(4):
            dve.wait_ge(g.wx_hi_made, n + 1)
            cols = slice(n * 2 * D, (n + 1) * 2 * D)
            sub(ffn_lo[:, cols], wx_raw[:, cols], f(ffn_hi[:, cols])).then_inc(g.wx_lo_made, 1)
        dve.wait_ge(g.vectors_loaded, 7 * 16)
        for l in range(DEPTH):
            last = nc.vector.tensor_tensor(rot_scaled[:, l, :, :, :], rot_scaled[:, l, :, :, :], rot_tab[:, :, :, :], ALU.mult)
        last.then_inc(g.rot_scaled_made, 1)

        def x_step(p):
            head, tail = p + 1, p + (-1)
            heads, tails, here = head.within(0, PAIRS), tail.within(0, PAIRS), p.within(0, PAIRS)
            for q in range(QPP):
                if q < QPP - 1 and here:
                    x_max(p, q + 1)
                if q == QPP - 1 and heads:
                    x_max(head, 0)
                if q == 0 and tails:
                    x_p2_part(tail, QPP - 1)
                if q > 0 and here:
                    x_p2_part(p, q - 1)
                if heads and q == 1:
                    x_low(head, zT_lo, zT_hi, bank[0][:, :], g.zT_hi_ready, g.zT_lo_ready, g.Q_ready)
                    x_low(head, cT_lo, cT_hi, bank[1][:, :], g.cT_hi_ready, g.cT_lo_ready, g.V_ready)
                if tails and q == 1:
                    x_normalise(tail, 1)
                if (p + (-2)).within(0, PAIRS) and q == 2:
                    y_first(p + (-2))
                if heads and q in (3, 4):
                    n = q - 3
                    dve.wait_ge((g.q32_ready, g.k32_ready)[n], head.times(1, 1))
                    wait(dve, g.xscores_ready, head.times(QPP, -QPP))
                    src, dst = (q32, k32)[n], (Q_hi, K_hi)[n][head.slot]
                    copy(flat(dst), flat(src)).then_inc((g.Q_hi_ready, g.K_hi_ready)[n], 1)
                if (head + 1).within(1, PAIRS) and q == 2:
                    ln_stats(head + 1)
                if here and q == 5:
                    x_normalise(p, 0)
                if tails and q == 5:
                    x_oT_low(tail)
                if (head + 1).within(1, PAIRS) and q == 5:
                    ln_apply(head + 1)
                if heads and q == 6:
                    dve.wait_ge(g.V_hi_ready, head.times(1, 1))
                    wait(dve, g.xPV_ready, head.times(QPP, -QPP))
                    sub(V_lo[head.slot][:, :, :, 0:XD].rearrange("p b h n -> p (b h) n"),
                        bank[1][:, :].rearrange("p (h n) -> p h n", n=XD),
                        V_hi[head.slot][:, :, :, 0:XD].rearrange("p b h n -> p (b h) n")).then_inc(g.V_lo_ready, 1)
                if tails and q == 7:
                    x_residual(tail)

        run_steps(dve, x_step, -1, PAIRS + 1, 2, PAIRS - 3)

        def att_hT(a, t0):
            dve.wait_ge(g.hT_hi_ready, a.times(1, t0 + 1))
            wait(dve, g.v_ready, a.times(1, t0 - 1))
            sub(hT_out(hT_lo[a.slot]), bank[7][:, 0:D].rearrange("p (c t) -> p c t", c=C2),
                f(hT_out(hT_hi[a.slot]))).then_inc(g.hT_lo_ready, 1)

        def att_rotate(a, t0, l, n):
            wait(dve, g.qk_sum, a.times(2, 2 * t0 + n - 1))
            v = bank[n][:, :].rearrange("p (h u d) -> p h u d", h=H, u=2)
            tab = rot_scaled[:, l, n, :, :].rearrange("p f (u d) -> p f u d", u=2)
            nc.vector.tensor_tensor(qk_a[:, n, :].rearrange("p (h d) -> p h d", h=H),
                                    bank[n][:, :].rearrange("p (h d) -> p h d", h=H),
                                    broadcast(rot_scaled[:, l, n, 0, :].unsqueeze(1), [P, H, HD]), ALU.mult)
            last = nc.vector.tensor_tensor(qk_b[:, n, :].rearrange("p (h u d) -> p h u d", h=H, u=2), v[:, :, ::-1, :],
                                           broadcast(tab[:, 1, :, :].unsqueeze(1), [P, H, 2, HD // 2]), ALU.mult)
            last.then_inc(g.qk_ab_ready, 1)

        def att_sums(a, t0, n):
            dve.wait_ge(g.squares_ready, a.times(2, 2 * t0 + n + 1))
            wait(dve, g.rnorm_ready, a.times(2, 2 * t0 + n - 1))
            nc.vector.tensor_reduce(ss[:, n, :], squares[:, n, :].rearrange("p (h d) -> p h d", h=H), AX.X,
                                    ALU.add).then_inc(g.sums_done, 1)

        def att_v(a, t0):
            dve.wait_ge(g.v_hi_ready, a.times(1, t0 + 1))
            sub(v_lo[a.slot][:, :, 0:HD], bank[2][:, :].rearrange("p (h n) -> p h n", h=H),
                v_hi[a.slot][:, :, 0:HD]).then_inc(g.v_lo_ready, 1)

        def att_qk_lo(t, t0, h):
            dve.wait_ge(g.qk_hi_ready, t.times(2, 2 * t0 + h + 1))
            v = bank[3][:, :].rearrange("p (n j t) -> p n j t", n=2, j=2)
            for e in range(2):
                rows = slice(64 * e, 64 * e + 64)
                sub(qm_lo[t.slot][h][rows, :, e, :], v[rows, 0, :, :], f(qm_hi[t.slot][h][rows, :, e, :]))
            sub(k_lo[t.slot][h][:, :, :], v[:, 1, :, :], f(k_hi[t.slot][h][:, :, :])).then_inc(g.qk_lo_ready, 1)

        def att_max(t, t0, h):
            dve.wait_ge(g.guess_ready, t.times(2, 2 * t0 + h + 1))
            nc.vector.tensor_reduce(nm[t.slot][h][:, :], bank[4][:, :].rearrange("p (i t) -> p i t", i=4), AX.X,
                                    ALU.max, negate=True).then_inc(g.max_ready, 1)

        def att_p2(t, t0, h):
            dve.wait_ge(g.p1_ready, t.times(2, 2 * t0 + h + 1))
            sub(p2[h][:, :, :], E[h][:, :, :], p1[h][:, :, :]).then_inc(g.p2_ready, 1)

        def att_normalise(t, t0, h):
            dve.wait_ge(g.PV_ready, t.times(2, 2 * t0 + h + 1))
            v = bank[6][:, 0:4 * (HD + 1)].rearrange("p (h n) -> p h n", h=4)
            nc.vector.reciprocal(rinv[:, h, :], v[:, :, HD:HD + 1].squeeze(2)).then_inc(g.rinv_ready, 1)
            dve.wait_ge(g.rinv_ready, t.times(2, 2 * t0 + h + 1))
            wait(dve, g.OT_ready, t.times(1, t0))
            nc.vector.tensor_tensor(O[:, 4 * h * HD:4 * (h + 1) * HD].rearrange("p (h n) -> p h n", h=4), v[:, :, 0:HD],
                                    broadcast(rinv[:, h, :].unsqueeze(2), [P, 4, HD]), ALU.mult).then_inc(g.O_ready, 1)

        def att_oT(t, t0):
            dve.wait_ge(g.OT_hi_ready, t.times(1, t0 + 1))
            wait(dve, g.att_out_ready, t.times(1, t0))
            sub(OT_lo[:, :, :].rearrange("p c t -> p (c t)"), bank[7][:, :],
                f(OT_hi[:, :, :]).rearrange("p c t -> p (c t)")).then_inc(g.OT_lo_ready, 1)

        def att_residual(t, t0):
            dve.wait_ge(g.att_out_ready, t.times(1, t0 + 1))
            y = y_all[:, bass.ds(t.times(1), 1), :].squeeze(1)
            nc.vector.tensor_tensor(y, bank[7][:, 0:D], y, ALU.add).then_inc(g.y_att_ready, 1)

        def att_step(t0, l):
            def body(i):
                a, b, c, d = i + 2, i + 1, i, i + (-1)
                on = lambda t: t.within(0, B)
                if on(c):
                    att_qk_lo(c, t0, 1)
                if on(a):
                    att_hT(a, t0)
                if on(d):
                    att_normalise(d, t0, 1)
                if on(c):
                    att_max(c, t0, 1)
                if on(b):
                    att_v(b, t0)
                if on(c):
                    att_p2(c, t0, 0)
                if on(a):
                    att_sums(a, t0, 0)
                if on(d):
                    att_oT(d, t0)
                if on(a):
                    att_rotate(a, t0, l, 0)
                if on(b):
                    att_qk_lo(b, t0, 0)
                if on(a):
                    att_sums(a, t0, 1)
                if on(c):
                    att_normalise(c, t0, 0)
                if on(b):
                    att_max(b, t0, 0)
                if on(c):
                    att_p2(c, t0, 1)
                if on(d):
                    att_residual(d, t0)
                if on(a):
                    att_rotate(a, t0, l, 1)
            return body

        def ffn_stats(gr, n, l):
            dve.wait_ge(g.y_shifted, gr * (16 * GT) + 16 * GT)
            wait_apart(dve, g.fz_ready, gr, g.wait_carried)
            for t in range(GT):
                nc.vector.bn_stats(bn[:, t, 0, :], y_all[:, bass.ds(n * GT + t, 1), 0:P].squeeze(1))
                last = nc.vector.bn_stats(bn[:, t, 1, :], y_shift[:, bass.ds(n * GT + t, 1), :].squeeze(1))
            last.then_inc(g.fbn_done, 1)
            wait_apart(dve, g.fbn_done, gr + 1, g.wait_carried)
            for t in range(GT):
                last = nc.vector.bn_aggr(mv[:, t, :], bn[:, t, :, :].rearrange("p a b -> p (a b)"))
            last.then_inc(g.fvar_ready, 1)

        def ffn_normalise(gr, n):
            dve.wait_ge(g.frstd_ready, gr + 1)
            wait(dve, g.fzT_ready, gr * 2)
            for t in range(GT):
                nc.vector.tensor_scalar(z4[:, t, 0:P], y_all[:, bass.ds(n * GT + t, 1), 0:P].squeeze(1),
                                        mv[:, t, 0:1], rstd[:, t:t + 1], ALU.subtract, ALU.mult)
                last = nc.vector.tensor_scalar(z4[:, t, P:D], y_shift[:, bass.ds(n * GT + t, 1), :].squeeze(1),
                                               mv[:, t, 0:1], rstd[:, t:t + 1], ALU.subtract, ALU.mult)
            last.then_inc(g.fz_ready, 1)

        def ffn_zT(gr):
            for c in range(C2):
                dve.wait_ge(g.fzT_hi_ready, gr * 2 + (c + 1))
                if c == 0:
                    wait(dve, g.h_ready, gr * (MFULL + 1))
                sub(zf_lo[:, c, :], bank[c][:, :], f(zf_hi[:, c, :])).then_inc(g.fzT_lo_ready, 1)

        def ffn_gate(gr, m, l):
            dve.wait_ge(g.gelu_ready, gr * (MFULL + 1) + (m + 1))
            if m >= 2:
                dve.wait_ge(g.u_lo_ready, gr * (MFULL + 1) + (m - 1))
            rows = slice(0, P if m < MFULL else 64)
            nc.vector.scalar_tensor_tensor(u32[m % 2][rows, :], bank[2 + 2 * (m % 2)][rows, :], b1_sb[rows, l, 2 * m:2 * m + 1],
                                           gel[m % 2][rows, :], ALU.add, ALU.mult).then_inc(g.u_ready, 1)

        def ffn_u_lo(gr, m):
            dve.wait_ge(g.u_hi_ready, gr * (MFULL + 1) + (m + 1))
            if m == 0:
                wait(dve, g.ffn_out_ready, gr * 2 + FIRST)
            rows = slice(0, P if m < MFULL else 64)
            sub(u_lo[rows, m, :], u32[m % 2][rows, :], f(u_hi[rows, m, :])).then_inc(g.u_lo_ready, 1)

        def ffn_residual(gr, n):
            dve.wait_ge(g.b2_added, gr + 1)
            for i in range(2):
                dve.wait_ge(g.ffn_out_ready, gr * 2 + (i + 1 + FIRST))
                y = tiles_of(y_all, n * GT + 2 * i, 2)
                nc.vector.tensor_tensor(y, bank[6 + i][:, :].rearrange("p (t n) -> p t n", t=2), y,
                                        ALU.add).then_inc(g.y_ffn_ready, 1)

        def ffn_group(gr, n, l):
            for m in range(MFULL + 1):
                ffn_gate(gr, m, l)
                if m > 0:
                    ffn_u_lo(gr, m - 1)
            ffn_u_lo(gr, MFULL)

        for l in range(DEPTH):
            t0, g0 = TILE0[l], GRP0[l]
            if l > 0:
                dve.wait_ge(g.y_ffn_ready, 2 * GRP0[l] + FIRST)
            else:
                dve.wait_ge(g.xout_ready, PAIRS)
                for i in range(2):
                    for t in (hT_hi, hT_lo):
                        nc.vector.memset(f(t[i][:, P + 1:P + 2]), 0.0)
                    nc.vector.memset(v_hi[i][:, :, HD:HD + 1], 1.0)
                    last = nc.vector.memset(v_lo[i][:, :, HD:HD + 1], 0.0)
                last.then_inc(g.zeros_made, 1)
                nc.vector.memset(y_shift[0:1, :, :], 0.0).then_inc(g.shift_zero, 1)
                dve.wait_ge(g.shift_zero, 1)
            if l == 0:
                dve.wait_ge(g.y_ready, PAIRS)
                dve.wait_ge(g.rot_scaled_made, 1)
            step = att_step(t0, l)
            step(Step(-SKEW))
            step(Step(-1))
            dve.wait_ge(g.b1_product, l + 1)
            nc.vector.tensor_tensor(b1_sb[:, l, :], bank[6][:, 0:NM], b1_sb[:, l, :], ALU.add).then_inc(g.b1_made, 1)
            for c in range(C2):
                cols = slice(c * NM * P, (c + 1) * NM * P)
                last = nc.vector.tensor_scalar(stage[:, cols], stage[:, cols], ln_sb[:, l, 0, c:c + 1], None, ALU.mult)
            last.then_inc(g.w1_scaled, 1)
            run_steps(dve, step, 0, B, 2, B - 5)
            dve.wait_ge(g.y_att_ready, t0 + B)
            ffn_stats(g0, 0, l)
            ffn_normalise(g0, 0)
            ffn_zT(g0)
            with dve.Fori(0, GROUPS - 1) as j:
                ffn_stats(j + (g0 + 1), j + 1, l)
                ffn_normalise(j + (g0 + 1), j + 1)
                ffn_group(j + g0, j, l)
                ffn_zT(j + (g0 + 1))
                ffn_residual(j + g0, j)
            ffn_group(g0 + GROUPS - 1, GROUPS - 1, l)
            ffn_residual(g0 + GROUPS - 1, GROUPS - 1)

    @block.gpsimd
    def _(pool):
        nc.gpsimd.memset(causal32[:, :, :], 0.0).then_inc(g.causal_made, 1)
        pool.wait_ge(g.causal_made, 1)
        nc.gpsimd.affine_select(out=causal32[:, :, :], in_=causal32[:, :, :], compare_op=ALU.is_ge, fill=-3.0e38, base=0,
                                pattern=[[0, 4], [-1, P]], channel_multiplier=1).then_inc(g.causal_made, 1)
        nc.gpsimd.memset(neg_half[:, :], -0.5).then_inc(g.zeros_a, 1)
        pool.wait_ge(g.zeros_a, 1)

        pool.wait_ge(g.consts_loaded, 16)

        def masked(dst, src, e):
            return nc.gpsimd.tensor_scalar(dst[:, :, :, e, :].rearrange("p c b t -> p (c b) t"),
                                           src.rearrange("p c b t -> p (c b) t"), const_sb[:, P + e:P + e + 1], 1.0,
                                           ALU.mult, ALU.mult)

        def ln_power(h, out_ap, var, ready, eps_done, done):
            wait_apart(pool, ready, h.times(1, 1), g.wait_carried)
            nc.gpsimd.tensor_scalar(out_ap, var, LN_EPS, 1.0, ALU.add, ALU.mult).then_inc(eps_done, 1)
            pool.wait_ge(eps_done, h.times(1, 1))
            nc.gpsimd.tensor_tensor(out_ap, out_ap, neg_half[:, 0:2], ALU.pow).then_inc(done, 1)

        def split_weights(hi, lo, cols_at, n, s_hi, s_made, count):
            nc.gpsimd.tensor_copy(hi[:, bass.ds(cols_at, n)], stage[:, bass.ds(cols_at, n)]).then_inc(s_hi, 1)
            pool.wait_ge(s_hi, count)
            nc.gpsimd.tensor_tensor(lo[:, bass.ds(cols_at, n)], stage[:, bass.ds(cols_at, n)],
                                    f(hi[:, bass.ds(cols_at, n)]), ALU.subtract).then_inc(s_made, 1)

        ln_power(Step(0), rstd[:, 0:2], mv[:, 0:2, 1:2].squeeze(2), g.var_ready, g.eps_added, g.rstd_ready)

        def x_step(p):
            head, tail = p + 1, p + (-1)
            heads, tails, here = head.within(0, PAIRS), tail.within(0, PAIRS), p.within(0, PAIRS)
            if (p + (-2)).within(0, PAIRS):
                ln_power(p + (-2), rstd2[:, 0:2], mv2[:, :, 1:2].squeeze(2), g.var2_ready, g.eps2_added, g.rstd2_ready)
            if here:
                pool.wait_ge(g.z_ready, p.times(1, 1))
                pair = tiles_of(x_all, p.times(2), 2)
                nc.gpsimd.tensor_tensor(pair, pair, broadcast(bo_sb[:, :].unsqueeze(1), [P, 2, D]), ALU.add).then_inc(g.bo_added, 1)
            if (head + 1).within(1, PAIRS):
                ln_power(head + 1, rstd[:, 0:2], mv[:, 0:2, 1:2].squeeze(2), g.var_ready, g.eps_added, g.rstd_ready)
            if heads:
                n = head.slot
                pool.wait_ge(g.Q_hi_ready, head.times(1, 1))
                nc.gpsimd.tensor_tensor(q_lo[:, :, :, :], q32[:, :, :, :], f(Q_hi[n][:, :, :, :]), ALU.subtract).then_inc(g.q_lo_ready, 1)
                for e in range(2):
                    masked(QM_hi[n], f(Q_hi[n][:, :, :, :]), e)
                wait_apart(pool, g.K_hi_ready, head.times(1, 1), g.wait_carried)
                masked(KM_hi[n], f(K_hi[n][:, :, :, :]), 0)
                masked(KM_hi[n], f(K_hi[n][:, :, :, :]), 1).then_inc(g.KM_ready, 1)
                nc.gpsimd.tensor_tensor(K_lo[n][:, :, :, :], k32[:, :, :, :], f(K_hi[n][:, :, :, :]), ALU.subtract).then_inc(g.K_lo_ready, 1)
                wait_apart(pool, g.q_lo_ready, head.times(1, 1), g.wait_carried)
                masked(QM_lo[n], q_lo[:, :, :, :], 0)
                masked(QM_lo[n], q_lo[:, :, :, :], 1).then_inc(g.QM_ready, 1)
            if here:
                split_weights(att_hi, att_lo, p.times(WATT // PAIRS), WATT // PAIRS, g.att_w_hi, g.att_w_made, p.times(1, 1))
            if p.j is None and p.c == PAIRS - 1:
                pool.wait_ge(g.V_ready, PAIRS)
                pool.wait_ge(g.QM_ready, PAIRS)
                for t in (qm_hi, qm_lo):
                    for i in range(2):
                        for h in range(2):
                            last = nc.gpsimd.memset(f(t[i][h][:, :, :, :]), 0.0)
                last.then_inc(g.qm_zeros_made, 1)
        x_step(Step(-1))
        pool.wait_ge(g.watt_loaded, 16)
        run_steps(pool, x_step, 0, PAIRS + 1, 2, PAIRS - 3)

        def att_rnorm(a, t0, n):
            wait_apart(pool, g.sums_done, a.times(2, 2 * t0 + n + 1), g.wait_carried)
            nc.gpsimd.tensor_scalar(ss[:, n, :], ss[:, n, :], NORM_FLOOR2, 1.0, ALU.max, ALU.mult).then_inc(g.ss_ready, 1)
            pool.wait_ge(g.ss_ready, a.times(2, 2 * t0 + n + 1))
            wait(pool, g.qk_ready, a.times(2, 2 * t0 + n - 1))
            nc.gpsimd.tensor_tensor(rnorm[:, n, :], ss[:, n, :], neg_half[:, 0:H], ALU.pow).then_inc(g.rnorm_ready, 1)

        def att_qk_sum(a, t0, n):
            pool.wait_ge(g.qk_ab_ready, a.times(2, 2 * t0 + n + 1))
            wait(pool, g.qkT_ready, a.times(2, 2 * t0 - 2))
            nc.gpsimd.tensor_tensor(qk[a.slot][:, n, :], qk_a[:, n, :], qk_b[:, n, :], ALU.add).then_inc(g.qk_sum, 1)

        def att_qk_scale(a, t0, n):
            pool.wait_ge(g.qk_sum, a.times(2, 2 * t0 + n + 1))
            pool.wait_ge(g.rnorm_ready, a.times(2, 2 * t0 + n + 1))
            v = qk[a.slot][:, n, :].rearrange("p (h d) -> p h d", h=H)
            nc.gpsimd.tensor_tensor(v, v, broadcast(rnorm[:, n, :].unsqueeze(2), [P, H, HD]), ALU.mult).then_inc(g.qk_ready, 1)

        def att_mask(t, t0, h):
            wait_apart(pool, g.exp_done, t.times(2, 2 * t0 + h + 1), g.wait_carried)
            nc.gpsimd.affine_select(out=E[h][:, :, :], in_=E[h][:, :, :], compare_op=ALU.is_ge, fill=0.0, base=0,
                                    pattern=[[0, 4], [1, P]], channel_multiplier=-1).then_inc(g.E_ready, 1)

        def att_step(t0):
            def body(i):
                a, b, c, d = i + 2, i + 1, i, i + (-1)
                on = lambda t: t.within(0, B)
                if on(c):
                    att_mask(c, t0, 0)
                if on(b):
                    att_qk_sum(b, t0, 1)
                    att_qk_scale(b, t0, 1)
                if on(d):
                    n = WFFN // B
                    cols = bass.ds(d.times(n), n)
                    pool.wait_ge(g.ffn_w_hi, d.times(1, t0 + 1))
                    nc.gpsimd.tensor_tensor(ffn_lo[:, cols], stage[:, cols], f(ffn_hi[:, cols]), ALU.subtract).then_inc(g.ffn_w_made, 1)
                if on(a):
                    att_rnorm(a, t0, 0)
                    att_qk_sum(a, t0, 0)
                if on(c):
                    att_mask(c, t0, 1)
                if on(a):
                    att_qk_scale(a, t0, 0)
                    att_rnorm(a, t0, 1)
            return body

        def ffn_power(gr):
            wait_apart(pool, g.fvar_ready, gr + 1, g.wait_carried)
            nc.gpsimd.tensor_scalar(rstd[:, :], mv[:, :, 1:2].squeeze(2), LN_EPS, 1.0, ALU.add, ALU.mult).then_inc(g.feps_added, 1)
            pool.wait_ge(g.feps_added, gr + 1)
            nc.gpsimd.tensor_tensor(rstd[:, :], rstd[:, :], neg_half[:, 0:GT], ALU.pow).then_inc(g.frstd_ready, 1)

        def ffn_bias(gr, n, l):
            pool.wait_ge(g.fz_ready, gr + 1)
            y = tiles_of(y_all, n * GT, GT)
            last = nc.gpsimd.tensor_tensor(y, y, broadcast(b2_sb[:, l, :].unsqueeze(1), [P, GT, D]), ALU.add)
            if l == DEPTH - 1:
                last.then_inc(g.b2_first, 1)
                pool.wait_ge(g.b2_first, n + 1)
                last = nc.gpsimd.tensor_tensor(y, y, tiles_of(x_all, n * GT, GT), ALU.add)
            last.then_inc(g.b2_added, 1)

        for l in range(DEPTH):
            t0, g0 = TILE0[l], GRP0[l]
            step = att_step(t0)
            for c in range(-SKEW, 1):
                step(Step(c))
            pool.wait_ge(g.w1_scaled, l + 1)
            run_steps(pool, step, 1, B, 2, B - 5)
            ffn_power(g0)
            with pool.Fori(0, GROUPS - 1) as j:
                ffn_power(j + (g0 + 1))
                ffn_bias(j + g0, j, l)
                if l + 1 < DEPTH:
                    n = WATT // GROUPS
                    if l == 0:
                        pool.wait_ge(g.watt_loaded, 32)
                    split_weights(att_hi, att_lo, j * n, n, g.att_w_hi, g.att_w_made, j + (PAIRS + 1))
            ffn_bias(g0 + GROUPS - 1, GROUPS - 1, l)
            if l + 1 < DEPTH:
                split_weights(att_hi, att_lo, (GROUPS - 1) * n, n, g.att_w_hi, g.att_w_made, PAIRS + GROUPS)

    held.close()


def constants():
    half = np.arange(0, HD, 2, dtype=np.float32)
    inv_freq = (1.0 / 10000.0 ** (half / HD)).astype(np.float32)
    t = np.arange(S, dtype=np.float32)
    freqs = np.concatenate([t[:, None] * inv_freq[None, :]] * 2, axis=-1).astype(np.float32)
    base = (half + np.float32(0.4 * HD)) / np.float32(1.4 * HD)
    power = (t - S // 2) / np.float32(128 // 2)
    scale = np.concatenate([base[None, :] ** power[:, None]] * 2, axis=-1).astype(np.float32)
    cos, sin = np.cos(freqs), np.sin(freqs)
    sign = np.concatenate([-np.ones(HD // 2), np.ones(HD // 2)]).astype(np.float32)
    qk_scale = np.float32(8.0)
    rot = np.stack([np.stack([cos * scale * qk_scale, sin * scale * sign * qk_scale], 1),
                    np.stack([cos / scale, sin / scale * sign], 1)], 1).astype(np.float32)
    consts = np.zeros((P, P + 2), np.float32)
    consts[:, :P] = np.eye(P)
    consts[:, P] = (np.arange(P) // XD) % 2 == 0
    consts[:, P + 1] = (np.arange(P) // XD) % 2 == 1
    return np.ascontiguousarray(rot), consts


def kernel(**inputs):
    import concourse.bacc as _bacc
    from concourse.bass_utils import run_bass_kernel_spmd as _run

    a = {k: np.asarray(v) for k, v in inputs.items()}
    rot, consts = constants()

    def rows_to_partitions(w):
        return w.reshape(-1, P, w.shape[1]).transpose(1, 0, 2).reshape(P, -1)

    def columns(v):
        return v.reshape(-1, P).T

    wx = np.concatenate([rows_to_partitions(a[f"L0_xattn_W{n}_w"].T) for n in "qkvo"], axis=1)
    bx = np.stack([columns(a[f"L0_xattn_W{n}_b"]) for n in "qkv"], axis=1)
    watt = np.stack([np.concatenate([rows_to_partitions(a["L0_ffn_wqkv"][l]), rows_to_partitions(a["L0_ffn_wo"][l])], axis=1)
                     for l in range(DEPTH)])

    def chunked(w):
        n = w.shape[0]
        va, vg = w[:, :HID], w[:, HID:]
        out = np.zeros((n, NM, P), w.dtype)
        out[:, 0:2 * MFULL:2] = va[:, :MFULL * P].reshape(n, MFULL, P)
        out[:, 1:2 * MFULL:2] = vg[:, :MFULL * P].reshape(n, MFULL, P)
        out[:, -1, 0:TAIL] = va[:, MFULL * P:]
        out[:, -1, 64:64 + TAIL] = vg[:, MFULL * P:]
        return out

    def padded(w):
        out = np.zeros(((MFULL + 1) * P, D), w.dtype)
        out[:HID] = w
        return out

    wffn = np.stack([np.concatenate([rows_to_partitions(chunked(a["L0_ffn_w1"][l]).reshape(D, NM * P)),
                                     rows_to_partitions(padded(a["L0_ffn_w2"][l]))], axis=1) for l in range(DEPTH)])
    b1 = chunked(a["L0_ffn_b1"]).transpose(2, 0, 1)
    lng = np.stack([np.stack([columns(a[n][l]) for n in ("L0_ffn_ln_g", "L0_ffn_ln_b")], 1) for l in range(DEPTH)], 1)
    scales = np.stack([np.stack([a[n], np.roll(a[n], HD // 2, axis=1)], 1) for n in ("L0_ffn_q_scale", "L0_ffn_k_scale")], 1)

    data = {"x": a["x"], "ctx": a["ctx_1024"], "wx": wx, "bx": bx, "bo": a["L0_xattn_Wo_b"], "watt": watt,
            "scales": scales, "rot": rot, "wffn": wffn, "lng": lng, "b1": b1, "b2": a["L0_ffn_b2"], "consts": consts}
    nc = _bacc.Bacc("TRN2", target_bir_lowering=False, num_devices=1)
    arrays, args = {}, []
    for name, v in data.items():
        v = np.ascontiguousarray(v)
        arrays[f"in_{name}"] = v
        args.append(nc.dram_tensor(f"in_{name}", v.shape, mybir.dt.from_np(v.dtype), kind="ExternalInput").ap())
    args.append(nc.dram_tensor("out_0", (B, S, D), mybir.dt.float32, kind="ExternalOutput").ap())
    program(nc, *args)
    r = _run(nc, [arrays], core_ids=[0])
    return r.results[0]["out_0"]
```

```python
import concourse.bass as bass
from concourse import mybir
from concourse.alu_op_type import AluOpType as ALU
from contextlib import ExitStack
import numpy as np

B, S, D = 16, 128, 256
P = 128
C2 = D // P
XH, XD = 16, 16
DEPTH, H, HD = 2, 8, 64
INNER = H * HD
C4 = INNER // P
HID = int(D * 4 * 2 / 3)
MFULL = HID // P
TAIL = HID - MFULL * P
NM = 2 * MFULL + 1
PAIRS = B // 2
QPB = 4
QPP = 2 * QPB
WQKV = C2 * 3 * INNER
WATT = WQKV + C4 * D
W1N = C2 * NM * P
WFFN = W1N + (MFULL + 1) * D
GT = 4
GROUPS = B // GT
SKEW = 2
LN_EPS = 1e-5
NORM_FLOOR2 = 1e-24


class Step:

    def __init__(self, c, j=None):
        self.c, self.j = c, j

    def __add__(self, n):
        return Step(self.c + n, self.j)

    @property
    def slot(self):
        return self.c % 2

    def times(self, k, plus=0):
        return k * self.c + plus if self.j is None else self.j * (2 * k) + (k * self.c + plus)

    def half(self, k, plus=0):
        return k * (self.c // 2) + plus if self.j is None else self.j * k + (k * (self.c // 2) + plus)

    def within(self, lo, hi):
        return self.j is not None or lo <= self.c < hi


class Signals:

    def __init__(self, sem):
        self.consts_loaded = sem("consts_loaded")
        self.x_first_loaded = sem("x_first_loaded")
        self.x_rest_loaded = sem("x_rest_loaded")
        self.wx_loaded = sem("wx_loaded")
        self.watt_loaded = sem("watt_loaded")
        self.wffn_loaded = sem("wffn_loaded")
        self.ctx0_loaded = sem("ctx0_loaded")
        self.ctx1_loaded = sem("ctx1_loaded")
        self.vectors_loaded = sem("vectors_loaded")
        self.y_shifted = sem("y_shifted")
        self.stored = sem("stored")
        self.wait_carried = sem("wait_carried")
        self.ident_bf_made = sem("ident_bf_made")
        self.fills_made = sem("fills_made")
        self.causal_made = sem("causal_made")
        self.rot_scaled_made = sem("rot_scaled_made")
        self.wx_hi_made = sem("wx_hi_made")
        self.wx_lo_made = sem("wx_lo_made")
        self.att_w_hi = sem("att_w_hi")
        self.att_w_made = sem("att_w_made")
        self.ffn_w_hi = sem("ffn_w_hi")
        self.ffn_w_made = sem("ffn_w_made")
        self.zeros_a = sem("zeros_a")
        self.qm_zeros_made = sem("qm_zeros_made")
        self.shift_zero = sem("shift_zero")
        self.bn_done = sem("bn_done")
        self.var_ready = sem("var_ready")
        self.eps_added = sem("eps_added")
        self.rstd_ready = sem("rstd_ready")
        self.z_ready = sem("z_ready")
        self.zT_ready = sem("zT_ready")
        self.cT_ready = sem("cT_ready")
        self.zT_hi_ready = sem("zT_hi_ready")
        self.cT_hi_ready = sem("cT_hi_ready")
        self.zT_lo_ready = sem("zT_lo_ready")
        self.cT_lo_ready = sem("cT_lo_ready")
        self.Q_ready = sem("Q_ready")
        self.K_ready = sem("K_ready")
        self.V_ready = sem("V_ready")
        self.q32_ready = sem("q32_ready")
        self.k32_ready = sem("k32_ready")
        self.Q_hi_ready = sem("Q_hi_ready")
        self.K_hi_ready = sem("K_hi_ready")
        self.q_lo_ready = sem("q_lo_ready")
        self.QM_ready = sem("QM_ready")
        self.K_lo_ready = sem("K_lo_ready")
        self.KM_ready = sem("KM_ready")
        self.V_hi_ready = sem("V_hi_ready")
        self.V_lo_ready = sem("V_lo_ready")
        self.xrinv_ready = sem("xrinv_ready")
        self.xO_ready = sem("xO_ready")
        self.xOT_ready = sem("xOT_ready")
        self.xOT_hi_ready = sem("xOT_hi_ready")
        self.xOT_lo_ready = sem("xOT_lo_ready")
        self.xout_ready = sem("xout_ready")
        self.bo_added = sem("bo_added")
        self.x_ready = sem("x_ready")
        self.bn2_done = sem("bn2_done")
        self.var2_ready = sem("var2_ready")
        self.eps2_added = sem("eps2_added")
        self.rstd2_ready = sem("rstd2_ready")
        self.y_ready = sem("y_ready")
        self.xguess_ready = sem("xguess_ready")
        self.xmax_ready = sem("xmax_ready")
        self.xscores_ready = sem("xscores_ready")
        self.xE_ready = sem("xE_ready")
        self.xp1_ready = sem("xp1_ready")
        self.xp2_ready = sem("xp2_ready")
        self.xPV_ready = sem("xPV_ready")
        self.y_tile_ready = sem("y_tile_ready")
        self.yT_ready = sem("yT_ready")
        self.hT_hi_ready = sem("hT_hi_ready")
        self.hT_lo_ready = sem("hT_lo_ready")
        self.q_ready = sem("q_ready")
        self.k_ready = sem("k_ready")
        self.v_ready = sem("v_ready")
        self.squares_ready = sem("squares_ready")
        self.sums_done = sem("sums_done")
        self.ss_ready = sem("ss_ready")
        self.rnorm_ready = sem("rnorm_ready")
        self.qk_ab_ready = sem("qk_ab_ready")
        self.qk_sum = sem("qk_sum")
        self.qk_ready = sem("qk_ready")
        self.v_hi_ready = sem("v_hi_ready")
        self.v_lo_ready = sem("v_lo_ready")
        self.OT_ready = sem("OT_ready")
        self.OT_hi_ready = sem("OT_hi_ready")
        self.OT_lo_ready = sem("OT_lo_ready")
        self.att_out_ready = sem("att_out_ready")
        self.y_att_ready = sem("y_att_ready")
        self.qkT_ready = sem("qkT_ready")
        self.qk_hi_ready = sem("qk_hi_ready")
        self.qk_lo_ready = sem("qk_lo_ready")
        self.qk_bf_ready = sem("qk_bf_ready")
        self.guess_ready = sem("guess_ready")
        self.max_ready = sem("max_ready")
        self.scores_ready = sem("scores_ready")
        self.exp_done = sem("exp_done")
        self.E_ready = sem("E_ready")
        self.p1_ready = sem("p1_ready")
        self.p2_ready = sem("p2_ready")
        self.PV_ready = sem("PV_ready")
        self.rinv_ready = sem("rinv_ready")
        self.O_ready = sem("O_ready")
        self.fbn_done = sem("fbn_done")
        self.fvar_ready = sem("fvar_ready")
        self.feps_added = sem("feps_added")
        self.frstd_ready = sem("frstd_ready")
        self.b2_first = sem("b2_first")
        self.fz_ready = sem("fz_ready")
        self.fzT_ready = sem("fzT_ready")
        self.fzT_scaled = sem("fzT_scaled")
        self.fzT_hi_ready = sem("fzT_hi_ready")
        self.fzT_lo_ready = sem("fzT_lo_ready")
        self.h_ready = sem("h_ready")
        self.gelu_ready = sem("gelu_ready")
        self.u_ready = sem("u_ready")
        self.u_hi_ready = sem("u_hi_ready")
        self.u_lo_ready = sem("u_lo_ready")
        self.ffn_out_ready = sem("ffn_out_ready")
        self.y_ffn_ready = sem("y_ffn_ready")
        self.b2_added = sem("b2_added")


def wait(engine, semaphore, value):
    if not (isinstance(value, int) and value <= 0):
        engine.wait_ge(semaphore, value)


def wait_apart(engine, semaphore, value, carrier):
    wait(engine, semaphore, value)
    if not isinstance(value, int):
        engine.sem_inc(carrier, 1)


def run_steps(engine, body, first, last, loop_first, loop_last):
    for c in range(first, loop_first):
        body(Step(c))
    assert (loop_last - loop_first + 1) % 2 == 0
    with engine.Fori(0, (loop_last - loop_first + 1) // 2) as j:
        body(Step(loop_first, j))
        body(Step(loop_first + 1, j))
    for c in range(loop_last + 1, last + 1):
        body(Step(c))


def program(nc, x, ctx, wx, bx, bo, watt, scales, rot, wffn, lng, b1, b2, consts, out):
    fp32, f32r, bf16, fp16 = mybir.dt.float32, mybir.dt.float32r, mybir.dt.bfloat16, mybir.dt.float16
    ACT = mybir.ActivationFunctionType
    AX = mybir.AxisListType

    held = ExitStack()

    def sb(name, shape, dt=fp32, at=held):
        return at.enter_context(nc.sbuf_tensor(name, shape, dt))

    def sem(name):
        return held.enter_context(nc.semaphore(name))

    def f(ap):
        return ap.bitcast(fp32)

    x_dram = x.rearrange("b s d -> s b d")
    ctx_dram = ctx.rearrange("b s d -> s b d")
    out_dram = out.rearrange("b s d -> s b d")

    x_all = sb("x_all", [P, B, D])
    y_all = sb("y_all", [P, B, D])
    y_shift = sb("y_shift", [P, B, P])
    att_hi = sb("att_hi", [P, WATT], f32r)
    att_lo = sb("att_lo", [P, WATT], f32r)
    ffn_hi = sb("ffn_hi", [P, WFFN], f32r)
    ffn_lo = sb("ffn_lo", [P, WFFN], f32r)
    stage = sb("stage", [P, WFFN])
    rot_tab = sb("rot_tab", [P, 2, 2, HD])
    rot_scaled = sb("rot_scaled", [P, DEPTH, 2, 2, HD])
    bx_sb = sb("bx_sb", [P, 3, C2])
    bo_sb = sb("bo_sb", [P, D])
    b2_sb = sb("b2_sb", [P, DEPTH, D])
    ln_sb = sb("ln_sb", [P, DEPTH, 2, C2])
    b1_sb = sb("b1_sb", [P, DEPTH, NM])
    const_sb = sb("const_sb", [P, P + 2])
    ident = const_sb[:, 0:P]
    ident_bf = sb("ident_bf", [P, P], bf16)
    neg_half = sb("neg_half", [P, H * 2])
    causal = sb("causal", [P, 4, P], bf16)
    causal32 = sb("causal32", [P, 4, P])
    bn = sb("bn", [P, GT, 2, 6])
    mv = sb("mv", [P, GT, 2])
    rstd = sb("rstd", [P, GT])
    bn2 = sb("bn2", [P, 2, 6])
    mv2 = sb("mv2", [P, 2, 2])
    rstd2 = sb("rstd2", [P, 2])

    held_x = ExitStack()

    def sx(name, shape, dt=fp32):
        return sb(name, shape, dt, held_x)

    Q_hi, K_hi, K_lo, QM_hi, QM_lo, KM_hi, V_hi, V_lo = ([] for _ in range(8))
    for i in range(2):
        for t, n in ((Q_hi, "Q_hi"), (K_hi, "K_hi"), (K_lo, "K_lo")):
            t.append(sx(f"{n}{i}", [P, C2, 2, P], f32r))
        for t, n in ((QM_hi, "QM_hi"), (QM_lo, "QM_lo"), (KM_hi, "KM_hi")):
            t.append(sx(f"{n}{i}", [P, C2, 2, 2, P], f32r))
        V_hi.append(sx(f"V_hi{i}", [P, 2, XH, XD + 1], fp16))
        V_lo.append(sx(f"V_lo{i}", [P, 2, XH, XD + 1], fp16))
    xOT_hi, xOT_lo = (sx(n, [P, C2, 2, P], f32r) for n in ("xOT_hi", "xOT_lo"))
    x_nm = [sx(f"x_nm{i}", [P, 4], bf16) for i in range(2)]
    x_E = [y_shift[:, 4 * i:4 * i + 4, :] for i in range(4)]
    x_p1 = [sx(f"x_p1{i}", [P, 4, P], fp16) for i in range(4)]
    x_rinv = sx("x_rinv", [P, XH])
    x_O = sx("x_O", [P, 2, D])
    ctx_sb = [sx(f"ctx_sb{i}", [P, 2, D]) for i in range(2)]
    z_sb = sx("z_sb", [P, 2, D])
    zT_hi, zT_lo = (sx(n, [P, C2, 2, P], f32r) for n in ("zT_hi", "zT_lo"))
    cT_hi, cT_lo = (sx(n, [P, C2, 2, P], f32r) for n in ("cT_hi", "cT_lo"))
    q32, k32 = sx("q32", [P, C2, 2, P]), sx("k32", [P, C2, 2, P])
    q_lo = sx("q_lo", [P, C2, 2, P])
    x_p2 = [sx(f"x_p2{i}", [P, 4, P], fp16) for i in range(4)]
    held_x.close()

    held_a = ExitStack()

    def sa(name, shape, dt=fp32):
        return sb(name, shape, dt, held_a)

    y_tile = [sa(f"y_tile{i}", [P, D]) for i in range(2)]
    squares = sa("squares", [P, 2, INNER])
    ss = sa("ss", [P, 2, H])
    rnorm = sa("rnorm", [P, 2, H])
    qk_a = sa("qk_a", [P, 2, INNER])
    qk_b = sa("qk_b", [P, 2, INNER])
    qk = [sa(f"qk{i}", [P, 2, INNER]) for i in range(2)]
    k_hi = [[sa(f"k_hi{i}{h}", [P, 2, P], f32r) for h in range(2)] for i in range(2)]
    k_lo = [[sa(f"k_lo{i}{h}", [P, 2, P], f32r) for h in range(2)] for i in range(2)]
    qm_bf = sa("qm_bf", [P, 2, 2, P], bf16)
    k_bf = sa("k_bf", [P, 2, P], bf16)
    nm = [[sa(f"nm{i}{h}", [P, 4], bf16) for h in range(2)] for i in range(2)]
    E = [sa(f"E{h}", [P, 4, P]) for h in range(2)]
    p1 = [sa(f"p1{h}", [P, 4, P], fp16) for h in range(2)]
    p2 = [sa(f"p2{h}", [P, 4, P], fp16) for h in range(2)]
    rinv = sa("rinv", [P, 2, 4])
    O = sa("O", [P, INNER])
    OT_hi, OT_lo = (sa(n, [P, C4, P], f32r) for n in ("OT_hi", "OT_lo"))
    sa("set_off", [P, 592])
    v_hi = [sa(f"v_hi{i}", [P, H, HD + 1], fp16) for i in range(2)]
    v_lo = [sa(f"v_lo{i}", [P, H, HD + 1], fp16) for i in range(2)]
    hT_hi = [sa(f"hT_hi{i}", [P, 2 * (P + 2)], f32r) for i in range(2)]
    hT_lo = [sa(f"hT_lo{i}", [P, 2 * (P + 2)], f32r) for i in range(2)]
    qm_hi = [[sa(f"qm_hi{i}{h}", [P, 2, 2, P], f32r) for h in range(2)] for i in range(2)]
    qm_lo = [[sa(f"qm_lo{i}{h}", [P, 2, 2, P], f32r) for h in range(2)] for i in range(2)]
    held_a.close()

    held_f = ExitStack()

    def sf(name, shape, dt=fp32):
        return sb(name, shape, dt, held_f)

    z4 = sf("z4", [P, GT, D])
    zf32 = sf("zf32", [P, C2, GT * P])
    zf_hi, zf_lo = (sf(n, [P, C2, GT * P], f32r) for n in ("zf_hi", "zf_lo"))
    gel = [sf(f"gel{i}", [P, GT * P]) for i in range(2)]
    u32 = [sf(f"u32{i}", [P, GT * P]) for i in range(2)]
    u_hi, u_lo = (sf(n, [P, MFULL + 1, GT * P], f32r) for n in ("u_hi", "u_lo"))
    held_f.close()

    bank = [held.enter_context(nc.psum_tensor(f"bank{i}", [P, 512], fp32)) for i in range(8)]

    g = Signals(sem)

    block = held.enter_context(nc.Block())

    def wx_part(t, n, c):
        return t[:, (n * C2 + c) * D:(n * C2 + c + 1) * D]

    def wqkv_part(t, c, n):
        return t[:, c * 3 * INNER + n * INNER:c * 3 * INNER + (n + 1) * INNER]

    def wo_part(t, c):
        return t[:, WQKV + c * D:WQKV + (c + 1) * D]

    def w1_part(t, c, m):
        return t[:, (c * NM + m) * P:(c * NM + m + 1) * P]

    def w2_part(t, m):
        return t[:, W1N + m * D:W1N + (m + 1) * D]

    wx_raw = y_all[:, 8:16, :].rearrange("p b d -> p (b d)")

    def hT(t, c):
        return t[:, c * (P + 1):c * (P + 1) + P]

    def hT_out(t):
        return t[:, :].rearrange("p (c n) -> p c n", c=C2)[:, :, 0:P]

    def broadcast(ap, shape):
        return ap.to_broadcast(shape)

    def yT_bank(a):
        return bank[{0: 5, 1: 4}.get(a.c, 7) if a.j is None else 7]

    def qk_bank(a, n):
        return bank[3] if a.j is None and (a.c, n) == (0, 0) else bank[n]

    def tiles_of(t, first, n):
        return t[:, bass.ds(first, n), :]

    FIRST = 1
    TILE0 = [l * B for l in range(DEPTH)]
    GRP0 = [l * GROUPS for l in range(DEPTH)]

    @block.sync
    def _(sp):
        sp.dma_start(x_all[:, 0:2, :], x_dram[:, 0:2, :]).then_inc(g.x_first_loaded, 16)
        sp.dma_start(const_sb[:, :], consts).then_inc(g.consts_loaded, 16)
        sp.dma_start(wx_raw, wx).then_inc(g.wx_loaded, 16)
        sp.dma_start(ctx_sb[0][:, :, :], ctx_dram[:, 0:2, :]).then_inc(g.ctx0_loaded, 16)
        for dst, src in ((bx_sb[:, :, :], bx), (bo_sb[:, :], bo.partition_broadcast(P)),
                         (b2_sb[:, :, :], b2.partition_broadcast(P)), (ln_sb[:, :, :, :], lng),
                         (b1_sb[:, :, :], b1), (rot_tab[:, :, :, :], rot),
                         (rot_scaled[:, :, :, :, :], scales.partition_broadcast(P))):
            sp.dma_start(dst, src).then_inc(g.vectors_loaded, 16)
        sp.dma_start(x_all[:, 2:B, :], x_dram[:, 2:B, :]).then_inc(g.x_rest_loaded, 16)
        sp.dma_start(ctx_sb[1][:, :, :], ctx_dram[:, 2:4, :]).then_inc(g.ctx1_loaded, 16)
        sp.dma_start(stage[:, 0:WATT], watt[0]).then_inc(g.watt_loaded, 16)

        with sp.Fori(1, PAIRS // 2) as j:
            for slot in range(2):
                sp.wait_ge(g.cT_ready, j * 2 + (slot - 1))
                sp.dma_start(ctx_sb[slot][:, :, :], ctx_dram[:, bass.ds(j * 4 + 2 * slot, 2), :]
                             ).then_inc((g.ctx0_loaded, g.ctx1_loaded)[slot], 16)

        for l in range(DEPTH):
            sp.wait_ge(g.att_w_made, (l + 1) * PAIRS if l == 0 else PAIRS + GROUPS)
            sp.dma_start(stage[:, 0:WFFN], wffn[l]).then_inc(g.wffn_loaded, 16)
            with sp.Fori(0, B) as t:
                sp.wait_ge(g.y_att_ready, t + (TILE0[l] + 1))
                sp.dma_start(y_shift[1:P, bass.ds(t, 1), :], y_all[0:P - 1, bass.ds(t, 1), P:D]
                             ).then_inc(g.y_shifted, 16)
                wait_apart(sp, g.y_shifted, (t + (TILE0[l] + 1)) * 16, g.wait_carried)
            if l + 1 < DEPTH:
                sp.wait_ge(g.ffn_w_made, (l + 1) * B)
                sp.dma_start(stage[:, 0:WATT], watt[l + 1]).then_inc(g.watt_loaded, 16)
        with sp.Fori(0, 2 * GROUPS) as half:
            sp.wait_ge(g.y_ffn_ready, half + (2 * GRP0[DEPTH - 1] + 1 + FIRST))
            sp.dma_start(out_dram[:, bass.ds(half * (GT // 2), GT // 2), :], y_all[:, bass.ds(half * (GT // 2), GT // 2), :]
                         ).then_inc(g.stored, 16)
        sp.wait_ge(g.stored, 16 * 2 * GROUPS)

    @block.tensor
    def _(pe):
        def split_product(out_ap, l_hi, l_lo, r_hi, r_lo, first, last):
            nc.tensor.matmul(out_ap, l_hi, r_hi, start=first, stop=False)
            nc.tensor.matmul(out_ap, l_hi, r_lo, start=False, stop=False)
            return nc.tensor.matmul(out_ap, l_lo, r_hi, start=False, stop=last)

        def scores_less_max(out_ap, k_h, k_l, q_h, q_l, less):
            nc.tensor.matmul(out_ap, k_h, q_h, start=True, stop=False)
            for e in range(2):
                nc.tensor.matmul(out_ap[:, e, :], broadcast(less[:, e:e + 1], [P, P]), ident_bf[:, :],
                                 start=False, stop=False, skip_group_check=True)
            nc.tensor.matmul(out_ap, k_h, q_l, start=False, stop=False)
            return nc.tensor.matmul(out_ap, k_l, q_h, start=False, stop=True)

        def project_z(h):
            pe.wait_ge(g.z_ready, h.times(1, 1))
            if h.j is None:
                wait(pe, g.k32_ready, h.c)
            wait(pe, g.x_ready, h.times(1, -2))
            v = bank[0][:, :].rearrange("p (c b t) -> p c b t", c=C2, b=2)
            for b in range(2):
                for c in range(C2):
                    last = nc.tensor.transpose(v[:, c, b, :], z_sb[:, b, c * P:(c + 1) * P], ident)
            last.then_inc(g.zT_ready, 1)
            pe.wait_ge((g.ctx0_loaded, g.ctx1_loaded)[h.slot], h.half(16, 16))
            wait(pe, g.V_lo_ready, h.times(1))
            v = bank[1][:, :].rearrange("p (c b t) -> p c b t", c=C2, b=2)
            for b in range(2):
                for c in range(C2):
                    last = nc.tensor.transpose(v[:, c, b, :], ctx_sb[h.slot][:, b, c * P:(c + 1) * P], ident)
            last.then_inc(g.cT_ready, 1)

        def project_qk(h, n, to, t_hi, t_lo):
            v = bank[to][:, :].rearrange("p (o n) -> p o n", o=C2)
            for o in range(C2):
                for c in range(C2):
                    last = split_product(
                        v[:, o, :], wx_part(ffn_hi, n, c)[:, o * P:(o + 1) * P], wx_part(ffn_lo, n, c)[:, o * P:(o + 1) * P],
                        t_hi[:, c, :, :], t_lo[:, c, :, :], c == 0, c == C2 - 1)
            return last

        def project_q(h):
            if h.j is None and h.c == 0:
                pe.wait_ge(g.wx_lo_made, 4)
            pe.wait_ge(g.zT_lo_ready, h.times(1, 1))
            if h.j is None:
                wait(pe, g.q32_ready, h.c)
            wait(pe, g.xOT_lo_ready, h.times(1, -2))
            project_qk(h, 0, 2, zT_hi, zT_lo).then_inc(g.Q_ready, 1)

        def project_k(h):
            pe.wait_ge(g.cT_lo_ready, h.times(1, 1))
            pe.wait_ge(g.zT_lo_ready, h.times(1, 1))
            project_qk(h, 1, 0, cT_hi, cT_lo).then_inc(g.K_ready, 1)

        def project_v(h):
            pe.wait_ge(g.cT_lo_ready, h.times(1, 1))
            v = bank[1][:, :].rearrange("p (b n) -> p b n", b=2)
            for b in range(2):
                for c in range(C2):
                    last = split_product(v[:, b, :], cT_hi[:, c, b, :], cT_lo[:, c, b, :],
                                         wx_part(ffn_hi, 2, c), wx_part(ffn_lo, 2, c), c == 0, c == C2 - 1)
            last.then_inc(g.V_ready, 1)

        def x_guess(p, q):
            b, r, n = q // QPB, q % QPB, q % 2
            if q == 0:
                pe.wait_ge(g.Q_hi_ready, p.times(1, 1))
                pe.wait_ge(g.KM_ready, p.times(1, 1))
            v = bank[3 + n][:, :].rearrange("p (c n) -> p c n", c=C2)
            rows = slice(32 * r, 32 * r + 32)
            for c in range(C2):
                last = nc.tensor.matmul(v[:, c, :], Q_hi[p.slot][rows, c, b, :],
                                        KM_hi[p.slot][rows, c, b, :, :], start=True, stop=True)
            last.then_inc(g.xguess_ready, 1)

        def x_scores(p, q):
            b, r, n = q // QPB, q % QPB, q % 2
            if q == 0:
                pe.wait_ge(g.QM_ready, p.times(1, 1))
                pe.wait_ge(g.K_lo_ready, p.times(1, 1))
            pe.wait_ge(g.xmax_ready, p.times(QPP, q + 1))
            wait(pe, g.xE_ready, p.times(QPP, q - 1))
            v = bank[5 + n][:, :].rearrange("p (c e n) -> p c e n", c=C2, e=2)
            rows = slice(32 * r, 32 * r + 32)
            for c in range(C2):
                last = scores_less_max(
                    v[:, c, :, :], K_hi[p.slot][rows, c, b, :], K_lo[p.slot][rows, c, b, :],
                    QM_hi[p.slot][rows, c, b, :, :], QM_lo[p.slot][rows, c, b, :, :], x_nm[n][:, 2 * c:2 * c + 2])
            last.then_inc(g.xscores_ready, 1)

        def x_weighted(p, q):
            b, r, n = q // QPB, q % QPB, q % 4
            if q == 0:
                pe.wait_ge(g.V_lo_ready, p.times(1, 1))
            if r == 0:
                wait(pe, g.xO_ready, p.times(2, b))
            pe.wait_ge(g.xp2_ready, p.times(QPP, q + 1))
            v = bank[7][:, 0:XH * (XD + 1)].rearrange("p (h n) -> p h n", h=XH)
            for c in range(C2):
                for e in range(2):
                    h, i = c * 8 + 2 * r + e, 2 * c + e
                    nc.tensor.matmul(v[:, h, :], x_p1[n][:, i, :], V_hi[p.slot][:, b, h, :], start=True, stop=False)
                    nc.tensor.matmul(v[:, h, :], x_p1[n][:, i, :], V_lo[p.slot][:, b, h, :], start=False, stop=False)
                    last = nc.tensor.matmul(v[:, h, :], x_p2[n][:, i, :], V_hi[p.slot][:, b, h, :], start=False, stop=True)
            last.then_inc(g.xPV_ready, 1)

        def x_transpose_o(t, h):
            pe.wait_ge(g.xO_ready, t.times(2, 2))
            if h is not None:
                pe.wait_ge(g.q32_ready, h.times(1, 1))
            else:
                wait(pe, g.xOT_lo_ready, t.times(1))
            v = bank[2][:, :].rearrange("p (c b t) -> p c b t", c=C2, b=2)
            for b in range(2):
                for c in range(C2):
                    last = nc.tensor.transpose(v[:, c, b, :], x_O[:, b, c * P:(c + 1) * P], ident)
            last.then_inc(g.xOT_ready, 1)

        def x_output(t, h):
            pe.wait_ge(g.xOT_lo_ready, t.times(1, 1))
            if h is not None:
                pe.wait_ge(g.k32_ready, h.times(1, 1))
            else:
                wait(pe, g.x_ready, t.times(1))
            v = bank[0][:, :].rearrange("p (b n) -> p b n", b=2)
            for b in range(2):
                for c in range(C2):
                    last = split_product(v[:, b, :], xOT_hi[:, c, b, :], xOT_lo[:, c, b, :],
                                         wx_part(ffn_hi, 3, c), wx_part(ffn_lo, 3, c), c == 0, c == C2 - 1)
            last.then_inc(g.xout_ready, 1)

        pe.wait_ge(g.consts_loaded, 16)
        pe.wait_ge(g.ident_bf_made, 1)
        pe.wait_ge(g.fills_made, 1)

        def x_step(p):
            head, tail = p + 1, p + (-1)
            heads, tails = head.within(0, PAIRS), tail.within(0, PAIRS)
            here = p.within(0, PAIRS)
            hh = head if heads else None
            final = p.j is None and p.c == PAIRS
            for q in range(QPP):
                if q == 0 and final:
                    pe.wait_ge(g.xE_ready, PAIRS * QPP - 1)
                    att_transpose_y(Step(0), 0)
                    att_transpose_y(Step(1), 0)
                if q == 2 and final:
                    att_qk(Step(0), 0, 0)
                if q < 3 and tails:
                    x_weighted(tail, QPP - 3 + q)
                if q == 2 and final:
                    att_qk(Step(0), 0, 1)
                if q in (4, 5, 6) and here:
                    x_weighted(p, q - 3)
                if q < QPP - 1 and here:
                    x_guess(p, q + 1)
                if q == QPP - 1 and heads:
                    x_guess(head, 0)
                if here:
                    x_scores(p, q)
                if heads:
                    if q == 0:
                        project_z(head)
                    if q == 2:
                        project_q(head)
                    if q == 3:
                        project_k(head)
                    if q == 5:
                        project_v(head)
                if tails:
                    if q == 4:
                        x_transpose_o(tail, hh)
                    if q == 6:
                        x_output(tail, hh)
                if q in (3, 7) and here:
                    x_weighted(p, q - 3)


        def att_transpose_y(a, t0):
            pe.wait_ge(g.y_tile_ready, a.times(1, t0 + 1))
            if a.j is None and a.c == 2:
                wait(pe, g.y_ffn_ready, t0 // B * 2 * GROUPS + FIRST)
                wait(pe, g.x_ready, PAIRS)
            if a.j is None and a.c > 2:
                wait(pe, g.hT_lo_ready, t0 + a.c)
            wait(pe, g.y_att_ready, a.times(1, t0 - 1 - SKEW))
            for c in range(C2):
                last = nc.tensor.transpose(yT_bank(a)[:, c * P:(c + 1) * P], y_tile[a.slot][:, c * P:(c + 1) * P], ident)
            last.then_inc(g.yT_ready, 1)

        def project(a, n, to):
            for c in range(C2):
                last = split_product(to[:, :], hT(hT_hi[a.slot], c), hT(hT_lo[a.slot], c),
                                     wqkv_part(att_hi, c, n), wqkv_part(att_lo, c, n), c == 0, c == C2 - 1)
            return last

        def att_qk(a, t0, n):
            if n == 0:
                pe.wait_ge(g.hT_lo_ready, a.times(1, t0 + 1))
                if a.j is None and a.c == 0:
                    pe.wait_ge(g.att_w_made, PAIRS if t0 == 0 else PAIRS + GROUPS)
            if (a.c, n) == (1, 0) and a.j is None:
                pe.wait_ge(g.x_ready, PAIRS)
            wait(pe, g.qk_ab_ready, a.times(2, 2 * t0 + n - 1))
            project(a, n, qk_bank(a, n)).then_inc((g.q_ready, g.k_ready)[n], 1)

        def att_v(b, t0):
            wait(pe, g.v_lo_ready, b.times(1, t0))
            project(b, 2, bank[2]).then_inc(g.v_ready, 1)

        def att_transpose_qk(t, t0, h):
            if h == 0:
                pe.wait_ge(g.qk_ready, t.times(2, 2 * t0 + 2))
            if h == 1:
                pe.wait_ge(g.qk_lo_ready, t.times(2, 2 * t0 + h))
            v = bank[3][:, :].rearrange("p (n j t) -> p n j t", n=2, j=2)
            for n in range(2):
                for j in range(2):
                    cols = slice((2 * h + j) * P, (2 * h + j + 1) * P)
                    last = nc.tensor.transpose(v[:, n, j, :], qk[t.slot][:, n, cols], ident)
            last.then_inc(g.qkT_ready, 1)

        def att_guess(t, t0, h):
            pe.wait_ge(g.qk_bf_ready, t.times(2, 2 * t0 + h + 1))
            v = bank[4][:, :].rearrange("p (j e t) -> p j e t", j=2, e=2)
            for j in range(2):
                for e in range(2):
                    nc.tensor.matmul(v[:, j, e, :], qm_bf[:, j, e, :], k_bf[:, j, :], start=(j, e) == (0, 0), stop=False,
                                     skip_group_check=True)
            last = nc.tensor.matmul(bank[4][:, :], ident_bf[:, :], causal[:, :, :], start=False, stop=True,
                                    skip_group_check=True)
            last.then_inc(g.guess_ready, 1)

        def att_scores(t, t0, h):
            pe.wait_ge(g.qk_lo_ready, t.times(2, 2 * t0 + h + 1))
            pe.wait_ge(g.max_ready, t.times(2, 2 * t0 + h + 1))
            wait(pe, g.exp_done, t.times(2, 2 * t0 + h))
            v = bank[5][:, :].rearrange("p (j e t) -> p j e t", j=2, e=2)
            kh, kl, qh, ql = (x[t.slot][h] for x in (k_hi, k_lo, qm_hi, qm_lo))
            for j in range(2):
                last = scores_less_max(v[:, j, :, :], kh[:, j, :], kl[:, j, :], qh[:, j, :, :], ql[:, j, :, :],
                                       nm[t.slot][h][:, 2 * j:2 * j + 2])
            last.then_inc(g.scores_ready, 1)

        def att_weighted(t, t0, h):
            if h == 0:
                pe.wait_ge(g.v_lo_ready, t.times(1, t0 + 1))
            pe.wait_ge(g.p2_ready, t.times(2, 2 * t0 + h + 1))
            wait(pe, g.O_ready, t.times(2, 2 * t0 + h))
            v = bank[6][:, 0:4 * (HD + 1)].rearrange("p (h n) -> p h n", h=4)
            for i in range(4):
                vh, vl = v_hi[t.slot][:, 4 * h + i, :], v_lo[t.slot][:, 4 * h + i, :]
                nc.tensor.matmul(v[:, i, :], p1[h][:, i, :], vh, start=True, stop=False)
                nc.tensor.matmul(v[:, i, :], p1[h][:, i, :], vl, start=False, stop=False)
                last = nc.tensor.matmul(v[:, i, :], p2[h][:, i, :], vh, start=False, stop=True)
            last.then_inc(g.PV_ready, 1)

        def att_transpose_o(t, t0):
            pe.wait_ge(g.O_ready, t.times(2, 2 * t0 + 2))
            if (t + (1 + SKEW)).within(0, B):
                pe.wait_ge(g.hT_lo_ready, t.times(1, t0 + 4))
            else:
                wait(pe, g.y_att_ready, t.times(1, t0))
            for c in range(C4):
                last = nc.tensor.transpose(bank[7][:, c * P:(c + 1) * P], O[:, c * P:(c + 1) * P], ident)
            last.then_inc(g.OT_ready, 1)

        def att_output(t, t0, part):
            if part == 0:
                pe.wait_ge(g.OT_lo_ready, t.times(1, t0 + 1))
            for c in (2 * part, 2 * part + 1):
                last = split_product(bank[7][:, 0:D], OT_hi[:, c, :], OT_lo[:, c, :],
                                     wo_part(att_hi, c), wo_part(att_lo, c), c == 0, c == C4 - 1)
            if part == 1:
                last.then_inc(g.att_out_ready, 1)

        def att_step(t0):
            def body(i):
                a, b, c, d = i + 2, i + 1, i, i + (-1)
                on = lambda t: t.within(0, B)
                if on(c):
                    att_scores(c, t0, 0)
                if a.within(2, B):
                    att_transpose_y(a, t0)
                if on(d):
                    att_weighted(d, t0, 1)
                if on(b):
                    att_v(b, t0)
                if on(c):
                    att_guess(c, t0, 1)
                if on(a):
                    att_qk(a, t0, 0)
                if on(d):
                    att_transpose_o(d, t0)
                if i.j is None and i.c == B - 1:
                    ffn_transpose(t0 // GT)
                if on(a):
                    att_qk(a, t0, 1)
                if on(b):
                    att_transpose_qk(b, t0, 0)
                if on(c):
                    att_scores(c, t0, 1)
                    att_weighted(c, t0, 0)
                if on(d):
                    att_output(d, t0, 0)
                if on(b):
                    att_guess(b, t0, 0)
                    att_transpose_qk(b, t0, 1)
                if on(d):
                    att_output(d, t0, 1)
            return body

        def ffn_transpose(gr):
            pe.wait_ge(g.fz_ready, gr + 1)
            wait(pe, g.fzT_scaled, gr * 2)
            for c in range(C2):
                for t in range(GT):
                    last = nc.tensor.transpose(bank[c][:, t * P:(t + 1) * P], z4[:, t, c * P:(c + 1) * P], ident)
                last.then_inc(g.fzT_ready, 1)

        def ffn_ups(gr, chunks):
            for m in chunks:
                ffn_up(gr, m)

        def ffn_up(gr, m):
            a = 2 + 2 * (m % 2)
            if m == 0:
                pe.wait_ge(g.fzT_lo_ready, gr * 2 + 2)
            if m >= 2:
                pe.wait_ge(g.u_ready, gr * (MFULL + 1) + (m - 1))
            for k in range(2 if m < MFULL else 1):
                for c in range(C2):
                    w = [w1_part(t, c, 2 * m + k) for t in (ffn_hi, ffn_lo)]
                    last = split_product(bank[a + k][:, :], w[0], w[1], zf_hi[:, c, :], zf_lo[:, c, :], c == 0, c == C2 - 1)
            last.then_inc(g.h_ready, 1)

        def ffn_down(gr, t_end, i, between=None):
            if i == 0:
                pe.wait_ge(g.y_att_ready, t_end)
                wait(pe, g.y_ffn_ready, gr * 2 + FIRST)
            def tile_part(i, t, chunks):
                for m in chunks:
                    if (i, t) == (0, 0):
                        pe.wait_ge(g.u_lo_ready, gr * (MFULL + 1) + (m + 1))
                    rows = slice(0, P if m < MFULL else 64)
                    cols = slice((2 * i + t) * P, (2 * i + t + 1) * P)
                    last = split_product(bank[6 + i][:, t * D:(t + 1) * D], u_hi[rows, m, cols], u_lo[rows, m, cols],
                                         w2_part(ffn_hi, m)[rows, :], w2_part(ffn_lo, m)[rows, :], m == 0, m == MFULL)
                return last

            if i == 0:
                tile_part(0, 0, range(MFULL - 1))
                tile_part(1, 0, range(MFULL - 1))
                if between:
                    between()
            tile_part(i, 0, (MFULL - 1, MFULL))
            tile_part(i, 1, range(MFULL + 1)).then_inc(g.ffn_out_ready, 1)

        def att_first_qk(t0):
            att_transpose_y(Step(1), t0)
            att_qk(Step(0), t0, 0)
            att_qk(Step(0), t0, 1)

        run_steps(pe, x_step, -1, PAIRS, 2, PAIRS - 3)
        for l in range(DEPTH):
            t0, g0 = TILE0[l], GRP0[l]
            run_steps(pe, att_step(t0), -1, B - 1, 2, B - 5)
            final, end = Step(B - 1), g0 + GROUPS - 1
            pe.wait_ge(g.ffn_w_made, B * (l + 1))
            ffn_up(g0, 0)
            att_weighted(final, t0, 1)
            att_transpose_o(final, t0)
            ffn_up(g0, 1)
            att_output(final, t0, 0)
            att_output(final, t0, 1)
            with pe.Fori(0, GROUPS - 1) as j:
                ffn_ups(j + g0, range(2, MFULL + 1))
                ffn_down(j + g0, t0 + B, 0, lambda: ffn_transpose(j + (g0 + 1)))
                ffn_down(j + g0, t0 + B, 1)
                ffn_ups(j + (g0 + 1), range(2))
            ffn_ups(end, range(2, MFULL + 1))
            if l + 1 < DEPTH:
                att_transpose_y(Step(0), t0 + B)
                ffn_down(end, t0 + B, 0)
                att_first_qk(t0 + B)
                ffn_down(end, t0 + B, 1)
            else:
                ffn_down(end, t0 + B, 0)
                ffn_down(end, t0 + B, 1)

    @block.scalar
    def _(act):
        def copy(o, i):
            return nc.scalar.activation(o, i, ACT.Copy)

        act.wait_ge(g.wx_loaded, 16)
        for n in range(4):
            cols = slice(n * 2 * D, (n + 1) * 2 * D)
            copy(ffn_hi[:, cols], wx_raw[:, cols]).then_inc(g.wx_hi_made, 1)

        def x_exp(p, q):
            n = q % 4
            act.wait_ge(g.xscores_ready, p.times(QPP, q + 1))
            wait(act, g.xp2_ready, p.times(QPP, q - 3))
            nc.scalar.activation(x_E[n].rearrange("p i t -> p (i t)"), bank[5 + q % 2][:, :], ACT.Exp,
                                 scale=float(XD) ** -0.5).then_inc(g.xE_ready, 1)
            act.wait_ge(g.xE_ready, p.times(QPP, q + 1))
            wait(act, g.xPV_ready, p.times(QPP, q - 3))
            copy(x_p1[n][:, :, :], x_E[n]).then_inc(g.xp1_ready, 1)

        def x_step(p):
            head, tail = p + 1, p + (-1)
            heads, tails, here = head.within(0, PAIRS), tail.within(0, PAIRS), p.within(0, PAIRS)
            final = p.j is None and p.c == PAIRS
            for q in range(QPP):
                if final and q == 0:
                    act.wait_ge(g.qm_zeros_made, 1)
                    att_hT(Step(0), 0)
                if p.j is None and p.c == PAIRS - 1 and q == QPP - 2:
                    act.wait_ge(g.y_ready, PAIRS - 2)
                    y_copy(Step(0), 0)
                    y_copy(Step(1), 0)
                if final and q == 3:
                    att_squares(Step(0), 0, 0)
                    att_squares(Step(0), 0, 1)
                if heads and q == 1:
                    act.wait_ge(g.zT_ready, head.times(1, 1))
                    wait(act, g.Q_ready, head.times(1))
                    copy(zT_hi[:, :, :, :].rearrange("p c b t -> p (c b t)"), bank[0][:, :]).then_inc(g.zT_hi_ready, 1)
                    act.wait_ge(g.cT_ready, head.times(1, 1))
                    wait(act, g.V_ready, head.times(1))
                    copy(cT_hi[:, :, :, :].rearrange("p c b t -> p (c b t)"), bank[1][:, :]).then_inc(g.cT_hi_ready, 1)
                if heads and q in (3, 4):
                    n = q - 3
                    if p.j is None and p.c == -1:
                        act.wait_ge(g.vectors_loaded, 7 * 16)
                    act.wait_ge((g.Q_ready, g.K_ready)[n], head.times(1, 1))
                    if n == 0:
                        wait(act, g.q_lo_ready, head.times(1))
                    else:
                        wait(act, g.K_lo_ready, head.times(1))
                    for c in range(C2):
                        last = nc.scalar.activation((q32, k32)[n][:, c, :, :].rearrange("p b t -> p (b t)"),
                                                    bank[(2, 0)[n]][:, c * D:(c + 1) * D], ACT.Identity,
                                                    bias=bx_sb[:, n, c:c + 1])
                    last.then_inc((g.q32_ready, g.k32_ready)[n], 1)
                if tails and q == 5:
                    act.wait_ge(g.xOT_ready, tail.times(1, 1))
                    wait(act, g.xout_ready, tail.times(1))
                    for c in range(C2):
                        last = nc.scalar.activation(xOT_hi[:, c, :, :].rearrange("p b t -> p (b t)"),
                                                    bank[2][:, c * D:(c + 1) * D], ACT.Identity, bias=bx_sb[:, 2, c:c + 1])
                    last.then_inc(g.xOT_hi_ready, 1)
                if heads and q == 6:
                    act.wait_ge(g.V_ready, head.times(1, 1))
                    wait(act, g.xPV_ready, head.times(QPP, -QPP))
                    copy(V_hi[head.slot][:, :, :, 0:XD].rearrange("p b h n -> p (b h) n"),
                         bank[1][:, :].rearrange("p (h n) -> p h n", n=XD)).then_inc(g.V_hi_ready, 1)
                if here:
                    x_exp(p, q)


        def y_copy(a, t0):
            wait_apart(act, g.yT_ready, a.times(1, t0 - 1), g.wait_carried)
            copy(y_tile[a.slot][:, :], y_all[:, bass.ds(a.times(1), 1), :].squeeze(1)).then_inc(g.y_tile_ready, 1)

        def att_hT(a, t0):
            act.wait_ge(g.yT_ready, a.times(1, t0 + 1))
            wait(act, g.v_ready, a.times(1, t0 - 1))
            copy(hT_out(hT_hi[a.slot]), yT_bank(a)[:, 0:D].rearrange("p (c t) -> p c t", c=C2)).then_inc(g.hT_hi_ready, 1)

        def att_squares(a, t0, n):
            act.wait_ge((g.q_ready, g.k_ready)[n], a.times(1, t0 + 1))
            wait(act, g.sums_done, a.times(2, 2 * t0 + n - 1))
            nc.scalar.activation(squares[:, n, :], qk_bank(a, n)[:, :], ACT.Square).then_inc(g.squares_ready, 1)

        def att_v(a, t0):
            act.wait_ge(g.v_ready, a.times(1, t0 + 1))
            wait(act, g.PV_ready, a.times(2, 2 * t0 - 2))
            copy(v_hi[a.slot][:, :, 0:HD], bank[2][:, :].rearrange("p (h n) -> p h n", h=H)).then_inc(g.v_hi_ready, 1)

        def att_qk_hi(t, t0, h):
            act.wait_ge(g.qkT_ready, t.times(2, 2 * t0 + h + 1))
            wait(act, g.scores_ready, t.times(2, 2 * t0 + h - 3))
            v = bank[3][:, :].rearrange("p (n j t) -> p n j t", n=2, j=2)
            for e in range(2):
                rows = slice(64 * e, 64 * e + 64)
                copy(qm_hi[t.slot][h][rows, :, e, :], v[rows, 0, :, :])
            copy(k_hi[t.slot][h][:, :, :], v[:, 1, :, :]).then_inc(g.qk_hi_ready, 1)

        def att_qk_bf(t, t0, h):
            wait(act, g.guess_ready, t.times(2, 2 * t0 + h))
            act.wait_ge(g.qk_hi_ready, t.times(2, 2 * t0 + h + 1))
            copy(qm_bf[:, :, :, :], f(qm_hi[t.slot][h][:, :, :, :]))
            copy(k_bf[:, :, :], f(k_hi[t.slot][h][:, :, :])).then_inc(g.qk_bf_ready, 1)

        def att_exp(t, t0, h):
            act.wait_ge(g.scores_ready, t.times(2, 2 * t0 + h + 1))
            wait(act, g.p2_ready, t.times(2, 2 * t0 + h - 1))
            nc.scalar.activation(E[h][:, :, :].rearrange("p i t -> p (i t)"), bank[5][:, :], ACT.Exp).then_inc(g.exp_done, 1)

        def att_p1(t, t0, h):
            act.wait_ge(g.E_ready, t.times(2, 2 * t0 + h + 1))
            wait(act, g.PV_ready, t.times(2, 2 * t0 + h - 1))
            copy(p1[h][:, :, :], E[h][:, :, :]).then_inc(g.p1_ready, 1)

        def att_oT(t, t0):
            act.wait_ge(g.OT_ready, t.times(1, t0 + 1))
            wait(act, g.att_out_ready, t.times(1, t0))
            copy(OT_hi[:, :, :].rearrange("p c t -> p (c t)"), bank[7][:, :]).then_inc(g.OT_hi_ready, 1)

        def weights_high(c, t0):
            n = WFFN // B
            copy(ffn_hi[:, bass.ds(c.times(n), n)], stage[:, bass.ds(c.times(n), n)]).then_inc(g.ffn_w_hi, 1)

        def att_step(t0, l):
            def body(i):
                a, b, c, d = i + 2, i + 1, i, i + (-1)
                on = lambda t: t.within(0, B)
                if on(c):
                    att_qk_hi(c, t0, 1)
                    att_qk_bf(c, t0, 1)
                    att_exp(c, t0, 0)
                if on(a):
                    att_hT(a, t0)
                if (a + 1).within(2, B):
                    y_copy(a + 1, t0)
                if on(c):
                    weights_high(c, t0)
                if on(c):
                    att_p1(c, t0, 0)
                if on(b):
                    att_v(b, t0)
                if on(a):
                    att_squares(a, t0, 0)
                if on(d):
                    att_oT(d, t0)
                if on(a):
                    att_squares(a, t0, 1)
                if on(b):
                    att_qk_hi(b, t0, 0)
                    att_qk_bf(b, t0, 0)
                if i.j is None and i.c == B - 1:
                    ffn_hT(t0 // GT, l, (0,))
                if on(c):
                    att_exp(c, t0, 1)
                if i.j is None and i.c == B - 1:
                    ffn_hT(t0 // GT, l, (1,))
                if on(c):
                    att_p1(c, t0, 1)
            return body

        def ffn_hT(gr, l, chunks=range(C2)):
            for c in chunks:
                act.wait_ge(g.fzT_ready, gr * 2 + (c + 1))
                if c == 0:
                    wait(act, g.fzT_lo_ready, gr * 2)
                nc.scalar.activation(zf32[:, c, :], bank[c][:, :], ACT.Identity, bias=ln_sb[:, l, 1, c:c + 1],
                                     scale=ln_sb[:, l, 0, c:c + 1]).then_inc(g.fzT_scaled, 1)
                act.wait_ge(g.fzT_scaled, gr * 2 + (c + 1))
                if c == 0:
                    wait(act, g.h_ready, gr * (MFULL + 1))
                copy(zf_hi[:, c, :], zf32[:, c, :]).then_inc(g.fzT_hi_ready, 1)

        def ffn_gelu(gr, m, l):
            act.wait_ge(g.h_ready, gr * (MFULL + 1) + (m + 1))
            if m >= 2:
                act.wait_ge(g.u_ready, gr * (MFULL + 1) + (m - 1))
            a = 2 + 2 * (m % 2)
            if m < MFULL:
                src, dst, bias = bank[a + 1][:, :], gel[m % 2][:, :], b1_sb[:, l, 2 * m + 1:2 * m + 2]
            else:
                src, dst, bias = bank[a][64:P, :], gel[m % 2][0:64, :], b1_sb[64:P, l, 2 * m:2 * m + 1]
            nc.scalar.activation(dst, src, ACT.Gelu, bias=bias).then_inc(g.gelu_ready, 1)

        def ffn_u_hi(gr, m):
            act.wait_ge(g.u_ready, gr * (MFULL + 1) + (m + 1))
            if m == 0:
                wait(act, g.ffn_out_ready, gr * 2 + FIRST)
            rows = slice(0, P if m < MFULL else 64)
            copy(u_hi[rows, m, :], u32[m % 2][rows, :]).then_inc(g.u_hi_ready, 1)

        def ffn_group(gr, l):
            for m in range(MFULL + 1):
                ffn_gelu(gr, m, l)
                if m > 0:
                    ffn_u_hi(gr, m - 1)
            ffn_u_hi(gr, MFULL)

        run_steps(act, x_step, -1, PAIRS, 2, PAIRS - 3)
        act.wait_ge(g.qm_zeros_made, 2)
        for l in range(DEPTH):
            t0, g0 = TILE0[l], GRP0[l]
            step = att_step(t0, l)
            if l > 0:
                step(Step(-SKEW))
            step(Step(-1))
            act.wait_ge(g.wffn_loaded, 16 * (l + 1))
            step(Step(0))
            act.wait_ge(g.y_ready, PAIRS)
            act.wait_ge(g.y_ffn_ready, 2 * GRP0[l] + FIRST)
            run_steps(act, step, 1, B, 2, B - 5)
            with act.Fori(0, GROUPS - 1) as j:
                ffn_group(j + g0, l)
                ffn_hT(j + (g0 + 1), l)
            if l + 1 < DEPTH:
                act.wait_ge(g.y_ffn_ready, 2 * g0 + 2 + FIRST)
                y_copy(Step(0), t0 + B)
                y_copy(Step(1), t0 + B)
            ffn_group(g0 + GROUPS - 1, l)

    @block.vector
    def _(dve):
        def copy(o, i):
            return nc.vector.tensor_copy(o, i)

        def sub(o, a, b):
            return nc.vector.tensor_tensor(o, a, b, ALU.subtract)

        dve.wait_ge(g.consts_loaded, 16)
        copy(ident_bf[:, :], ident).then_inc(g.ident_bf_made, 1)
        for i in range(2):
            nc.vector.memset(V_hi[i][:, :, :, XD:XD + 1], 1.0).then_inc((g.y_ffn_ready, g.ffn_out_ready)[i], FIRST)
            last = nc.vector.memset(V_lo[i][:, :, :, XD:XD + 1], 0.0)
        last.then_inc(g.fills_made, 1)
        dve.wait_ge(g.causal_made, 2)
        copy(causal[:, :, :], causal32[:, :, :]).then_inc(g.causal_made, 1)

        def ln_stats(h):
            if h.j is None and h.c < 2:
                dve.wait_ge((g.x_first_loaded, g.x_rest_loaded)[h.c], 16)
            wait_apart(dve, g.z_ready, h.times(1), g.wait_carried)
            for b in range(2):
                last = nc.vector.bn_stats(bn[:, b, 0, :], x_all[:, bass.ds(h.times(2, b), 1), :].squeeze(1))
            last.then_inc(g.bn_done, 1)
            wait_apart(dve, g.bn_done, h.times(1, 1), g.wait_carried)
            for b in range(2):
                last = nc.vector.bn_aggr(mv[:, b, :], bn[:, b, 0, :])
            last.then_inc(g.var_ready, 1)

        def ln_apply(h):
            dve.wait_ge(g.rstd_ready, h.times(1, 1))
            wait(dve, g.zT_ready, h.times(1))
            for b in range(2):
                last = nc.vector.tensor_scalar(z_sb[:, b, :], x_all[:, bass.ds(h.times(2, b), 1), :].squeeze(1),
                                               mv[:, b, 0:1], rstd[:, b:b + 1], ALU.subtract, ALU.mult)
            last.then_inc(g.z_ready, 1)

        def flat(t):
            return t[:, :, :, :].rearrange("p c b t -> p (c b t)")

        def x_low(h, lo, hi, src, ready_hi, ready_lo, used):
            dve.wait_ge(ready_hi, h.times(1, 1))
            wait(dve, used, h.times(1))
            sub(flat(lo), src, f(flat(hi))).then_inc(ready_lo, 1)

        def x_max(p, q):
            n = q % 2
            dve.wait_ge(g.xguess_ready, p.times(QPP, q + 1))
            wait(dve, g.xscores_ready, p.times(QPP, q - 1))
            nc.vector.tensor_reduce(x_nm[n][:, :], bank[3 + n][:, :].rearrange("p (i t) -> p i t", i=4), AX.X,
                                    ALU.max, negate=True).then_inc(g.xmax_ready, 1)

        def x_p2_part(p, q):
            n = q % 4
            dve.wait_ge(g.xp1_ready, p.times(QPP, q + 1))
            wait(dve, g.xPV_ready, p.times(QPP, q - 3))
            sub(x_p2[n][:, :, :], x_E[n], x_p1[n][:, :, :]).then_inc(g.xp2_ready, 1)

        def x_normalise(p, b):
            dve.wait_ge(g.xPV_ready, p.times(QPP, QPB * (b + 1)))
            v = bank[7][:, 0:XH * (XD + 1)].rearrange("p (h n) -> p h n", h=XH)
            wait(dve, g.xO_ready, p.times(2, b))
            nc.vector.reciprocal(x_rinv[:, :], v[:, :, XD:XD + 1].squeeze(2)).then_inc(g.xrinv_ready, 1)
            dve.wait_ge(g.xrinv_ready, p.times(2, b + 1))
            wait(dve, g.xOT_ready, p.times(1))
            nc.vector.tensor_tensor(x_O[:, b, :].rearrange("p (h n) -> p h n", h=XH), v[:, :, 0:XD],
                                    broadcast(x_rinv[:, :].unsqueeze(2), [P, XH, XD]), ALU.mult).then_inc(g.xO_ready, 1)

        def x_oT_low(t):
            dve.wait_ge(g.xOT_hi_ready, t.times(1, 1))
            wait(dve, g.xout_ready, t.times(1))
            for c in range(C2):
                last = nc.vector.scalar_tensor_tensor(
                    xOT_lo[:, c, :, :].rearrange("p b t -> p (b t)"), bank[2][:, c * D:(c + 1) * D], bx_sb[:, 2, c:c + 1],
                    f(xOT_hi[:, c, :, :]).rearrange("p b t -> p (b t)"), ALU.add, ALU.subtract)
            last.then_inc(g.xOT_lo_ready, 1)

        def x_residual(t):
            dve.wait_ge(g.xout_ready, t.times(1, 1))
            dve.wait_ge(g.bo_added, t.times(1, 1))
            pair = tiles_of(x_all, t.times(2), 2)
            nc.vector.tensor_tensor(pair, bank[0][:, :].rearrange("p (b n) -> p b n", b=2), pair,
                                    ALU.add).then_inc(g.x_ready, 1)
            dve.wait_ge(g.x_ready, t.times(1, 1))
            wait_apart(dve, g.y_ready, t.times(1), g.wait_carried)
            for b in range(2):
                last = nc.vector.bn_stats(bn2[:, b, :], x_all[:, bass.ds(t.times(2, b), 1), :].squeeze(1))
            last.then_inc(g.bn2_done, 1)
            wait_apart(dve, g.bn2_done, t.times(1, 1), g.wait_carried)
            for b in range(2):
                last = nc.vector.bn_aggr(mv2[:, b, :], bn2[:, b, :])
            last.then_inc(g.var2_ready, 1)

        def y_first(t):
            dve.wait_ge(g.rstd2_ready, t.times(1, 1))
            for b in range(2):
                last = nc.vector.tensor_scalar(y_all[:, bass.ds(t.times(2, b), 1), :].squeeze(1),
                                               x_all[:, bass.ds(t.times(2, b), 1), :].squeeze(1),
                                               mv2[:, b, 0:1], rstd2[:, b:b + 1], ALU.subtract, ALU.mult)
            last.then_inc(g.y_ready, 1)

        ln_stats(Step(0))
        ln_apply(Step(0))
        for n in range(4):
            dve.wait_ge(g.wx_hi_made, n + 1)
            cols = slice(n * 2 * D, (n + 1) * 2 * D)
            sub(ffn_lo[:, cols], wx_raw[:, cols], f(ffn_hi[:, cols])).then_inc(g.wx_lo_made, 1)
        dve.wait_ge(g.vectors_loaded, 7 * 16)
        for l in range(DEPTH):
            last = nc.vector.tensor_tensor(rot_scaled[:, l, :, :, :], rot_scaled[:, l, :, :, :], rot_tab[:, :, :, :], ALU.mult)
        last.then_inc(g.rot_scaled_made, 1)

        def x_step(p):
            head, tail = p + 1, p + (-1)
            heads, tails, here = head.within(0, PAIRS), tail.within(0, PAIRS), p.within(0, PAIRS)
            final = p.j is None and p.c == PAIRS
            for q in range(QPP):
                if q < QPP - 1 and here:
                    x_max(p, q + 1)
                if q == QPP - 1 and heads:
                    x_max(head, 0)
                if q == 0 and tails:
                    x_p2_part(tail, QPP - 1)
                if q > 0 and here:
                    x_p2_part(p, q - 1)
                if heads and q == 1:
                    x_low(head, zT_lo, zT_hi, bank[0][:, :], g.zT_hi_ready, g.zT_lo_ready, g.Q_ready)
                    x_low(head, cT_lo, cT_hi, bank[1][:, :], g.cT_hi_ready, g.cT_lo_ready, g.V_ready)
                if final and q == 1:
                    dve.wait_ge(g.V_ready, PAIRS)
                    for i in range(2):
                        for t in (hT_hi, hT_lo):
                            nc.vector.memset(f(t[i][:, P + 1:P + 2]), 0.0)
                    att_hT(Step(0), 0)
                if tails and q == 2:
                    x_normalise(tail, 1)
                if final and q == 3:
                    att_sums(Step(0), 0, 0)
                    att_rotate(Step(0), 0, 0, 0)
                if (p + (-2)).within(0, PAIRS) and q == 2:
                    y_first(p + (-2))
                if heads and q in (3, 4):
                    n = q - 3
                    dve.wait_ge((g.q32_ready, g.k32_ready)[n], head.times(1, 1))
                    wait(dve, g.xscores_ready, head.times(QPP, -QPP))
                    src, dst = (q32, k32)[n], (Q_hi, K_hi)[n][head.slot]
                    copy(flat(dst), flat(src)).then_inc((g.Q_hi_ready, g.K_hi_ready)[n], 1)
                if (head + 1).within(1, PAIRS) and q == 2:
                    ln_stats(head + 1)
                if tails and q == 5:
                    x_oT_low(tail)
                if final and q == 5:
                    for i in range(2):
                        nc.vector.memset(v_hi[i][:, :, HD:HD + 1], 1.0)
                        nc.vector.memset(v_lo[i][:, :, HD:HD + 1], 0.0)
                    att_sums(Step(0), 0, 1)
                    att_rotate(Step(0), 0, 0, 1)
                if (head + 1).within(1, PAIRS) and q == 5:
                    ln_apply(head + 1)
                if here and q == 6:
                    x_normalise(p, 0)
                if heads and q == 6:
                    dve.wait_ge(g.V_hi_ready, head.times(1, 1))
                    wait(dve, g.xPV_ready, head.times(QPP, -QPP))
                    sub(V_lo[head.slot][:, :, :, 0:XD].rearrange("p b h n -> p (b h) n"),
                        bank[1][:, :].rearrange("p (h n) -> p h n", n=XD),
                        V_hi[head.slot][:, :, :, 0:XD].rearrange("p b h n -> p (b h) n")).then_inc(g.V_lo_ready, 1)
                if tails and q == 7:
                    x_residual(tail)


        def att_hT(a, t0):
            dve.wait_ge(g.hT_hi_ready, a.times(1, t0 + 1))
            wait(dve, g.v_ready, a.times(1, t0 - 1))
            sub(hT_out(hT_lo[a.slot]), yT_bank(a)[:, 0:D].rearrange("p (c t) -> p c t", c=C2),
                f(hT_out(hT_hi[a.slot]))).then_inc(g.hT_lo_ready, 1)

        def att_rotate(a, t0, l, n):
            wait(dve, g.qk_sum, a.times(2, 2 * t0 + n - 1))
            v = qk_bank(a, n)[:, :].rearrange("p (h u d) -> p h u d", h=H, u=2)
            tab = rot_scaled[:, l, n, :, :].rearrange("p f (u d) -> p f u d", u=2)
            nc.vector.tensor_tensor(qk_a[:, n, :].rearrange("p (h d) -> p h d", h=H),
                                    qk_bank(a, n)[:, :].rearrange("p (h d) -> p h d", h=H),
                                    broadcast(rot_scaled[:, l, n, 0, :].unsqueeze(1), [P, H, HD]), ALU.mult)
            last = nc.vector.tensor_tensor(qk_b[:, n, :].rearrange("p (h u d) -> p h u d", h=H, u=2), v[:, :, ::-1, :],
                                           broadcast(tab[:, 1, :, :].unsqueeze(1), [P, H, 2, HD // 2]), ALU.mult)
            last.then_inc(g.qk_ab_ready, 1)
            if a.j is None and a.c == 0:
                dve.wait_ge(g.qk_ab_ready, 2 * t0 + n + 1)
                nc.vector.tensor_tensor(qk[0][:, n, :], qk_a[:, n, :], qk_b[:, n, :], ALU.add).then_inc(g.qk_sum, 1)

        def att_sums(a, t0, n):
            dve.wait_ge(g.squares_ready, a.times(2, 2 * t0 + n + 1))
            wait(dve, g.rnorm_ready, a.times(2, 2 * t0 + n - 1))
            nc.vector.tensor_reduce(ss[:, n, :], squares[:, n, :].rearrange("p (h d) -> p h d", h=H), AX.X,
                                    ALU.add).then_inc(g.sums_done, 1)

        def att_v(a, t0):
            dve.wait_ge(g.v_hi_ready, a.times(1, t0 + 1))
            sub(v_lo[a.slot][:, :, 0:HD], bank[2][:, :].rearrange("p (h n) -> p h n", h=H),
                v_hi[a.slot][:, :, 0:HD]).then_inc(g.v_lo_ready, 1)

        def att_qk_lo(t, t0, h):
            dve.wait_ge(g.qk_hi_ready, t.times(2, 2 * t0 + h + 1))
            v = bank[3][:, :].rearrange("p (n j t) -> p n j t", n=2, j=2)
            for e in range(2):
                rows = slice(64 * e, 64 * e + 64)
                sub(qm_lo[t.slot][h][rows, :, e, :], v[rows, 0, :, :], f(qm_hi[t.slot][h][rows, :, e, :]))
            sub(k_lo[t.slot][h][:, :, :], v[:, 1, :, :], f(k_hi[t.slot][h][:, :, :])).then_inc(g.qk_lo_ready, 1)

        def att_max(t, t0, h):
            dve.wait_ge(g.guess_ready, t.times(2, 2 * t0 + h + 1))
            nc.vector.tensor_reduce(nm[t.slot][h][:, :], bank[4][:, :].rearrange("p (i t) -> p i t", i=4), AX.X,
                                    ALU.max, negate=True).then_inc(g.max_ready, 1)

        def att_p2(t, t0, h):
            dve.wait_ge(g.p1_ready, t.times(2, 2 * t0 + h + 1))
            sub(p2[h][:, :, :], E[h][:, :, :], p1[h][:, :, :]).then_inc(g.p2_ready, 1)

        def att_normalise(t, t0, h):
            dve.wait_ge(g.PV_ready, t.times(2, 2 * t0 + h + 1))
            v = bank[6][:, 0:4 * (HD + 1)].rearrange("p (h n) -> p h n", h=4)
            nc.vector.reciprocal(rinv[:, h, :], v[:, :, HD:HD + 1].squeeze(2)).then_inc(g.rinv_ready, 1)
            dve.wait_ge(g.rinv_ready, t.times(2, 2 * t0 + h + 1))
            wait(dve, g.OT_ready, t.times(1, t0))
            nc.vector.tensor_tensor(O[:, 4 * h * HD:4 * (h + 1) * HD].rearrange("p (h n) -> p h n", h=4), v[:, :, 0:HD],
                                    broadcast(rinv[:, h, :].unsqueeze(2), [P, 4, HD]), ALU.mult).then_inc(g.O_ready, 1)

        def att_oT(t, t0):
            dve.wait_ge(g.OT_hi_ready, t.times(1, t0 + 1))
            wait(dve, g.att_out_ready, t.times(1, t0))
            sub(OT_lo[:, :, :].rearrange("p c t -> p (c t)"), bank[7][:, :],
                f(OT_hi[:, :, :]).rearrange("p c t -> p (c t)")).then_inc(g.OT_lo_ready, 1)

        def att_residual(t, t0):
            dve.wait_ge(g.att_out_ready, t.times(1, t0 + 1))
            y = y_all[:, bass.ds(t.times(1), 1), :].squeeze(1)
            nc.vector.tensor_tensor(y, bank[7][:, 0:D], y, ALU.add).then_inc(g.y_att_ready, 1)

        def att_step(t0, l):
            def body(i):
                a, b, c, d = i + 2, i + 1, i, i + (-1)
                on = lambda t: t.within(0, B)
                if on(c):
                    att_qk_lo(c, t0, 1)
                if a.within(1, B):
                    att_hT(a, t0)
                if on(d):
                    att_normalise(d, t0, 1)
                if i.j is None and i.c == B - 1:
                    ffn_normalise(t0 // GT, 0, late)
                if on(c):
                    att_max(c, t0, 1)
                if on(b):
                    att_v(b, t0)
                if on(c):
                    att_p2(c, t0, 0)
                if on(a):
                    att_sums(a, t0, 0)
                if i.j is None and i.c == B - 2:
                    ffn_stats(t0 // GT, 0, late)
                if on(d):
                    att_oT(d, t0)
                if on(a):
                    att_rotate(a, t0, l, 0)
                if on(b):
                    att_qk_lo(b, t0, 0)
                if on(a):
                    att_sums(a, t0, 1)
                if i.j is None and i.c == B - 1:
                    ffn_zT(t0 // GT, (0,))
                if on(c):
                    att_normalise(c, t0, 0)
                if i.j is None and i.c == B - 1:
                    ffn_zT(t0 // GT, (1,))
                if on(b):
                    att_max(b, t0, 0)
                if on(c):
                    att_p2(c, t0, 1)
                if on(d):
                    att_residual(d, t0)
                if on(a):
                    att_rotate(a, t0, l, 1)
                if i.j is None and i.c == B - 3:
                    ffn_stats(t0 // GT, 0, early)
                if i.j is None and i.c == B - 2:
                    ffn_normalise(t0 // GT, 0, early)
            return body

        early, late = range(GT // 2), range(GT // 2, GT)

        def ffn_stats(gr, n, tiles=range(GT)):
            if tiles[0] == 0:
                dve.wait_ge(g.y_shifted, gr * (16 * GT) + 16 * GT)
                wait_apart(dve, g.fz_ready, gr, g.wait_carried)
            for t in tiles:
                nc.vector.bn_stats(bn[:, t, 0, :], y_all[:, bass.ds(n * GT + t, 1), 0:P].squeeze(1))
                last = nc.vector.bn_stats(bn[:, t, 1, :], y_shift[:, bass.ds(n * GT + t, 1), :].squeeze(1))
            if tiles[-1] == GT - 1:
                last.then_inc(g.fbn_done, 1)
                wait_apart(dve, g.fbn_done, gr + 1, g.wait_carried)
                for t in range(GT):
                    last = nc.vector.bn_aggr(mv[:, t, :], bn[:, t, :, :].rearrange("p a b -> p (a b)"))
                last.then_inc(g.fvar_ready, 1)

        def ffn_normalise(gr, n, tiles=range(GT)):
            if tiles[0] == 0:
                dve.wait_ge(g.frstd_ready, gr + 1)
                wait(dve, g.fzT_ready, gr * 2)
            for t in tiles:
                nc.vector.tensor_scalar(z4[:, t, 0:P], y_all[:, bass.ds(n * GT + t, 1), 0:P].squeeze(1),
                                        mv[:, t, 0:1], rstd[:, t:t + 1], ALU.subtract, ALU.mult)
                last = nc.vector.tensor_scalar(z4[:, t, P:D], y_shift[:, bass.ds(n * GT + t, 1), :].squeeze(1),
                                               mv[:, t, 0:1], rstd[:, t:t + 1], ALU.subtract, ALU.mult)
            if tiles[-1] == GT - 1:
                last.then_inc(g.fz_ready, 1)

        def ffn_zT(gr, chunks=range(C2)):
            for c in chunks:
                dve.wait_ge(g.fzT_hi_ready, gr * 2 + (c + 1))
                if c == 0:
                    wait(dve, g.h_ready, gr * (MFULL + 1))
                sub(zf_lo[:, c, :], zf32[:, c, :], f(zf_hi[:, c, :])).then_inc(g.fzT_lo_ready, 1)

        def ffn_gate(gr, m, l):
            dve.wait_ge(g.gelu_ready, gr * (MFULL + 1) + (m + 1))
            if m >= 2:
                dve.wait_ge(g.u_lo_ready, gr * (MFULL + 1) + (m - 1))
            rows = slice(0, P if m < MFULL else 64)
            nc.vector.scalar_tensor_tensor(u32[m % 2][rows, :], bank[2 + 2 * (m % 2)][rows, :], b1_sb[rows, l, 2 * m:2 * m + 1],
                                           gel[m % 2][rows, :], ALU.add, ALU.mult).then_inc(g.u_ready, 1)

        def ffn_u_lo(gr, m):
            dve.wait_ge(g.u_hi_ready, gr * (MFULL + 1) + (m + 1))
            if m == 0:
                wait(dve, g.ffn_out_ready, gr * 2 + FIRST)
            rows = slice(0, P if m < MFULL else 64)
            sub(u_lo[rows, m, :], u32[m % 2][rows, :], f(u_hi[rows, m, :])).then_inc(g.u_lo_ready, 1)

        def ffn_residual(gr, n, halves=range(2)):
            dve.wait_ge(g.b2_added, gr + 1)
            for i in halves:
                dve.wait_ge(g.ffn_out_ready, gr * 2 + (i + 1 + FIRST))
                y = tiles_of(y_all, n * GT + 2 * i, 2)
                nc.vector.tensor_tensor(y, bank[6 + i][:, :].rearrange("p (t n) -> p t n", t=2), y,
                                        ALU.add).then_inc(g.y_ffn_ready, 1)

        def ffn_group(gr, l, following=None):
            for m in range(MFULL + 1):
                ffn_gate(gr, m, l)
                if m > 0:
                    ffn_u_lo(gr, m - 1)
                if following and m in (0, 1):
                    ffn_stats(*following, (early, late)[m])
                if following and m in (2, 3):
                    ffn_normalise(*following, (early, late)[m - 2])
            ffn_u_lo(gr, MFULL)

        run_steps(dve, x_step, -1, PAIRS, 2, PAIRS - 3)
        for l in range(DEPTH):
            t0, g0 = TILE0[l], GRP0[l]
            end = g0 + GROUPS - 1
            step = att_step(t0, l)
            if l > 0:
                step(Step(-SKEW))
                ffn_residual(g0 - 1, GROUPS - 1, (1,))
            step(Step(-1))
            if l == 0:
                x_step(Step(PAIRS + 1))
                dve.wait_ge(g.shift_zero, 1)
            run_steps(dve, step, 0, B, 2, B - 5)
            with dve.Fori(0, GROUPS - 1) as j:
                ffn_group(j + g0, l, (j + (g0 + 1), j + 1))
                ffn_zT(j + (g0 + 1))
                ffn_residual(j + g0, j)
            ffn_group(end, l)
            if l + 1 < DEPTH:
                att_hT(Step(0), t0 + B)
                ffn_residual(end, GROUPS - 1, (0,))
            else:
                ffn_residual(end, GROUPS - 1)

    @block.gpsimd
    def _(pool):
        nc.gpsimd.memset(causal32[:, :, :], 0.0).then_inc(g.causal_made, 1)
        pool.wait_ge(g.causal_made, 1)
        nc.gpsimd.affine_select(out=causal32[:, :, :], in_=causal32[:, :, :], compare_op=ALU.is_ge, fill=-3.0e38, base=0,
                                pattern=[[0, 4], [-1, P]], channel_multiplier=1).then_inc(g.causal_made, 1)
        nc.gpsimd.memset(neg_half[:, :], -0.5).then_inc(g.zeros_a, 1)
        pool.wait_ge(g.zeros_a, 1)

        pool.wait_ge(g.consts_loaded, 16)

        def masked(dst, src, e):
            return nc.gpsimd.tensor_scalar(dst[:, :, :, e, :].rearrange("p c b t -> p (c b) t"),
                                           src.rearrange("p c b t -> p (c b) t"), const_sb[:, P + e:P + e + 1], 1.0,
                                           ALU.mult, ALU.mult)

        def ln_power(h, out_ap, var, ready, eps_done, done):
            wait_apart(pool, ready, h.times(1, 1), g.wait_carried)
            nc.gpsimd.tensor_scalar(out_ap, var, LN_EPS, 1.0, ALU.add, ALU.mult).then_inc(eps_done, 1)
            pool.wait_ge(eps_done, h.times(1, 1))
            nc.gpsimd.tensor_tensor(out_ap, out_ap, neg_half[:, 0:2], ALU.pow).then_inc(done, 1)

        def split_weights(hi, lo, cols_at, n, s_hi, s_made, count):
            nc.gpsimd.tensor_copy(hi[:, bass.ds(cols_at, n)], stage[:, bass.ds(cols_at, n)]).then_inc(s_hi, 1)
            pool.wait_ge(s_hi, count)
            nc.gpsimd.tensor_tensor(lo[:, bass.ds(cols_at, n)], stage[:, bass.ds(cols_at, n)],
                                    f(hi[:, bass.ds(cols_at, n)]), ALU.subtract).then_inc(s_made, 1)

        ln_power(Step(0), rstd[:, 0:2], mv[:, 0:2, 1:2].squeeze(2), g.var_ready, g.eps_added, g.rstd_ready)

        def x_step(p):
            head, tail = p + 1, p + (-1)
            heads, tails, here = head.within(0, PAIRS), tail.within(0, PAIRS), p.within(0, PAIRS)
            if (p + (-2)).within(0, PAIRS):
                ln_power(p + (-2), rstd2[:, 0:2], mv2[:, :, 1:2].squeeze(2), g.var2_ready, g.eps2_added, g.rstd2_ready)
            if here:
                pool.wait_ge(g.z_ready, p.times(1, 1))
                pair = tiles_of(x_all, p.times(2), 2)
                nc.gpsimd.tensor_tensor(pair, pair, broadcast(bo_sb[:, :].unsqueeze(1), [P, 2, D]), ALU.add).then_inc(g.bo_added, 1)
            if (head + 1).within(1, PAIRS):
                ln_power(head + 1, rstd[:, 0:2], mv[:, 0:2, 1:2].squeeze(2), g.var_ready, g.eps_added, g.rstd_ready)
            if heads:
                n = head.slot
                pool.wait_ge(g.Q_hi_ready, head.times(1, 1))
                nc.gpsimd.tensor_tensor(q_lo[:, :, :, :], q32[:, :, :, :], f(Q_hi[n][:, :, :, :]), ALU.subtract).then_inc(g.q_lo_ready, 1)
                for e in range(2):
                    masked(QM_hi[n], f(Q_hi[n][:, :, :, :]), e)
                wait_apart(pool, g.K_hi_ready, head.times(1, 1), g.wait_carried)
                masked(KM_hi[n], f(K_hi[n][:, :, :, :]), 0)
                masked(KM_hi[n], f(K_hi[n][:, :, :, :]), 1).then_inc(g.KM_ready, 1)
                nc.gpsimd.tensor_tensor(K_lo[n][:, :, :, :], k32[:, :, :, :], f(K_hi[n][:, :, :, :]), ALU.subtract).then_inc(g.K_lo_ready, 1)
                wait_apart(pool, g.q_lo_ready, head.times(1, 1), g.wait_carried)
                masked(QM_lo[n], q_lo[:, :, :, :], 0)
                masked(QM_lo[n], q_lo[:, :, :, :], 1).then_inc(g.QM_ready, 1)
            if here:
                split_weights(att_hi, att_lo, p.times(WATT // PAIRS), WATT // PAIRS, g.att_w_hi, g.att_w_made, p.times(1, 1))
            if p.j is None and p.c == PAIRS - 1:
                pool.wait_ge(g.V_ready, PAIRS)
                pool.wait_ge(g.QM_ready, PAIRS)
                for t in qm_buffers[:-1]:
                    last = nc.gpsimd.memset(f(t[:, :, :, :]), 0.0)
                last.then_inc(g.qm_zeros_made, 1)
        qm_buffers = [t[i][h] for t in (qm_hi, qm_lo) for i in range(2) for h in range(2)]
        x_step(Step(-1))
        pool.wait_ge(g.watt_loaded, 16)
        run_steps(pool, x_step, 0, PAIRS, 2, PAIRS - 3)
        pool.wait_ge(g.xp2_ready, PAIRS * QPP)
        nc.gpsimd.memset(y_shift[0:1, :, :], 0.0).then_inc(g.shift_zero, 1)
        pool.wait_ge(g.shift_zero, 1)
        pool.wait_ge(g.xPV_ready, PAIRS * QPP)
        nc.gpsimd.memset(f(qm_buffers[-1][:, :, :, :]), 0.0).then_inc(g.qm_zeros_made, 1)

        def att_rnorm(a, t0, n):
            wait_apart(pool, g.sums_done, a.times(2, 2 * t0 + n + 1), g.wait_carried)
            nc.gpsimd.tensor_scalar(ss[:, n, :], ss[:, n, :], NORM_FLOOR2, 1.0, ALU.max, ALU.mult).then_inc(g.ss_ready, 1)
            pool.wait_ge(g.ss_ready, a.times(2, 2 * t0 + n + 1))
            wait(pool, g.qk_ready, a.times(2, 2 * t0 + n - 1))
            nc.gpsimd.tensor_tensor(rnorm[:, n, :], ss[:, n, :], neg_half[:, 0:H], ALU.pow).then_inc(g.rnorm_ready, 1)

        def att_qk_sum(a, t0, n):
            if a.j is None and a.c == 0:
                return
            pool.wait_ge(g.qk_ab_ready, a.times(2, 2 * t0 + n + 1))
            wait(pool, g.qkT_ready, a.times(2, 2 * t0 - 2))
            nc.gpsimd.tensor_tensor(qk[a.slot][:, n, :], qk_a[:, n, :], qk_b[:, n, :], ALU.add).then_inc(g.qk_sum, 1)

        def att_qk_scale(a, t0, n):
            pool.wait_ge(g.qk_sum, a.times(2, 2 * t0 + n + 1))
            pool.wait_ge(g.rnorm_ready, a.times(2, 2 * t0 + n + 1))
            v = qk[a.slot][:, n, :].rearrange("p (h d) -> p h d", h=H)
            nc.gpsimd.tensor_tensor(v, v, broadcast(rnorm[:, n, :].unsqueeze(2), [P, H, HD]), ALU.mult).then_inc(g.qk_ready, 1)

        def att_mask(t, t0, h):
            wait_apart(pool, g.exp_done, t.times(2, 2 * t0 + h + 1), g.wait_carried)
            nc.gpsimd.affine_select(out=E[h][:, :, :], in_=E[h][:, :, :], compare_op=ALU.is_ge, fill=0.0, base=0,
                                    pattern=[[0, 4], [1, P]], channel_multiplier=-1).then_inc(g.E_ready, 1)

        def att_step(t0):
            def body(i):
                a, b, c = i + 2, i + 1, i
                on = lambda t: t.within(0, B)
                if on(c):
                    att_mask(c, t0, 0)
                if on(b):
                    att_qk_sum(b, t0, 1)
                    att_qk_scale(b, t0, 1)
                if on(c):
                    n = WFFN // B
                    cols = bass.ds(c.times(n), n)
                    pool.wait_ge(g.ffn_w_hi, c.times(1, t0 + 1))
                    nc.gpsimd.tensor_tensor(ffn_lo[:, cols], stage[:, cols], f(ffn_hi[:, cols]), ALU.subtract).then_inc(g.ffn_w_made, 1)
                if on(a):
                    att_rnorm(a, t0, 0)
                    att_qk_sum(a, t0, 0)
                if i.j is None and i.c == B - 2:
                    ffn_power(t0 // GT)
                if on(c):
                    att_mask(c, t0, 1)
                if on(a):
                    att_qk_scale(a, t0, 0)
                    att_rnorm(a, t0, 1)
            return body

        def ffn_power(gr):
            wait_apart(pool, g.fvar_ready, gr + 1, g.wait_carried)
            nc.gpsimd.tensor_scalar(rstd[:, :], mv[:, :, 1:2].squeeze(2), LN_EPS, 1.0, ALU.add, ALU.mult).then_inc(g.feps_added, 1)
            pool.wait_ge(g.feps_added, gr + 1)
            nc.gpsimd.tensor_tensor(rstd[:, :], rstd[:, :], neg_half[:, 0:GT], ALU.pow).then_inc(g.frstd_ready, 1)

        def ffn_bias(gr, n, l):
            pool.wait_ge(g.fz_ready, gr + 1)
            y = tiles_of(y_all, n * GT, GT)
            last = nc.gpsimd.tensor_tensor(y, y, broadcast(b2_sb[:, l, :].unsqueeze(1), [P, GT, D]), ALU.add)
            if l == DEPTH - 1:
                last.then_inc(g.b2_first, 1)
                pool.wait_ge(g.b2_first, n + 1)
                last = nc.gpsimd.tensor_tensor(y, y, tiles_of(x_all, n * GT, GT), ALU.add)
            last.then_inc(g.b2_added, 1)

        for l in range(DEPTH):
            t0, g0 = TILE0[l], GRP0[l]
            step = att_step(t0)
            step(Step(-SKEW))
            if l == 0:
                x_step(Step(PAIRS + 1))
            run_steps(pool, step, -1, B - 1, 2, B - 5)
            with pool.Fori(0, GROUPS - 1) as j:
                ffn_power(j + (g0 + 1))
                ffn_bias(j + g0, j, l)
                if l + 1 < DEPTH:
                    n = WATT // GROUPS
                    if l == 0:
                        pool.wait_ge(g.watt_loaded, 32)
                    split_weights(att_hi, att_lo, j * n, n, g.att_w_hi, g.att_w_made, j + (PAIRS + 1))
            ffn_bias(g0 + GROUPS - 1, GROUPS - 1, l)
            if l + 1 < DEPTH:
                split_weights(att_hi, att_lo, (GROUPS - 1) * n, n, g.att_w_hi, g.att_w_made, PAIRS + GROUPS)

    held.close()


def constants():
    half = np.arange(0, HD, 2, dtype=np.float32)
    inv_freq = (1.0 / 10000.0 ** (half / HD)).astype(np.float32)
    t = np.arange(S, dtype=np.float32)
    freqs = np.concatenate([t[:, None] * inv_freq[None, :]] * 2, axis=-1).astype(np.float32)
    base = (half + np.float32(0.4 * HD)) / np.float32(1.4 * HD)
    power = (t - S // 2) / np.float32(128 // 2)
    scale = np.concatenate([base[None, :] ** power[:, None]] * 2, axis=-1).astype(np.float32)
    cos, sin = np.cos(freqs), np.sin(freqs)
    sign = np.concatenate([-np.ones(HD // 2), np.ones(HD // 2)]).astype(np.float32)
    qk_scale = np.float32(8.0)
    rot = np.stack([np.stack([cos * scale * qk_scale, sin * scale * sign * qk_scale], 1),
                    np.stack([cos / scale, sin / scale * sign], 1)], 1).astype(np.float32)
    consts = np.zeros((P, P + 2), np.float32)
    consts[:, :P] = np.eye(P)
    consts[:, P] = (np.arange(P) // XD) % 2 == 0
    consts[:, P + 1] = (np.arange(P) // XD) % 2 == 1
    return np.ascontiguousarray(rot), consts


def kernel(**inputs):
    import concourse.bacc as _bacc
    from concourse.bass_utils import run_bass_kernel_spmd as _run

    a = {k: np.asarray(v) for k, v in inputs.items()}
    rot, consts = constants()

    def rows_to_partitions(w):
        return w.reshape(-1, P, w.shape[1]).transpose(1, 0, 2).reshape(P, -1)

    def columns(v):
        return v.reshape(-1, P).T

    wx = np.concatenate([rows_to_partitions(a[f"L0_xattn_W{n}_w"].T) for n in "qkvo"], axis=1)
    bx = np.stack([columns(a[f"L0_xattn_W{n}_b"]) for n in "qkv"], axis=1)
    watt = np.stack([np.concatenate([rows_to_partitions(a["L0_ffn_wqkv"][l]), rows_to_partitions(a["L0_ffn_wo"][l])], axis=1)
                     for l in range(DEPTH)])

    def chunked(w):
        n = w.shape[0]
        va, vg = w[:, :HID], w[:, HID:]
        out = np.zeros((n, NM, P), w.dtype)
        out[:, 0:2 * MFULL:2] = va[:, :MFULL * P].reshape(n, MFULL, P)
        out[:, 1:2 * MFULL:2] = vg[:, :MFULL * P].reshape(n, MFULL, P)
        out[:, -1, 0:TAIL] = va[:, MFULL * P:]
        out[:, -1, 64:64 + TAIL] = vg[:, MFULL * P:]
        return out

    def padded(w):
        out = np.zeros(((MFULL + 1) * P, D), w.dtype)
        out[:HID] = w
        return out

    wffn = np.stack([np.concatenate([rows_to_partitions(chunked(a["L0_ffn_w1"][l]).reshape(D, NM * P)),
                                     rows_to_partitions(padded(a["L0_ffn_w2"][l]))], axis=1) for l in range(DEPTH)])
    b1 = chunked(a["L0_ffn_b1"]).transpose(2, 0, 1)
    lng = np.stack([np.stack([columns(a[n][l]) for n in ("L0_ffn_ln_g", "L0_ffn_ln_b")], 1) for l in range(DEPTH)], 1)
    scales = np.stack([np.stack([a[n], np.roll(a[n], HD // 2, axis=1)], 1) for n in ("L0_ffn_q_scale", "L0_ffn_k_scale")], 1)

    data = {"x": a["x"], "ctx": a["ctx_1024"], "wx": wx, "bx": bx, "bo": a["L0_xattn_Wo_b"], "watt": watt,
            "scales": scales, "rot": rot, "wffn": wffn, "lng": lng, "b1": b1, "b2": a["L0_ffn_b2"], "consts": consts}
    nc = _bacc.Bacc("TRN2", target_bir_lowering=False, num_devices=1)
    arrays, args = {}, []
    for name, v in data.items():
        v = np.ascontiguousarray(v)
        arrays[f"in_{name}"] = v
        args.append(nc.dram_tensor(f"in_{name}", v.shape, mybir.dt.from_np(v.dtype), kind="ExternalInput").ap())
    args.append(nc.dram_tensor("out_0", (B, S, D), mybir.dt.float32, kind="ExternalOutput").ap())
    program(nc, *args)
    r = _run(nc, [arrays], core_ids=[0])
    return r.results[0]["out_0"]
```
